# Optimizing a Trainium2 kernel written in Bass

```python
import numpy as np
import jax
import jax.numpy as jnp

def _softmax(x, axis=-1):
    return jax.nn.softmax(x, axis=axis)

def _gelu(x):
    return jax.nn.gelu(x, approximate=True)

def _silu(x):
    return jax.nn.silu(x)

def _sigmoid(x):
    return jax.nn.sigmoid(x)

def _layernorm(x, axis=-1, eps=1e-05):
    m = jnp.mean(x, axis=axis, keepdims=True)
    v = jnp.var(x, axis=axis, keepdims=True)
    return (x - m) / jnp.sqrt(v + eps)

def _scatter_add(tgt, idx, src, axis=0):
    return tgt.at[idx].add(src)

def _segment_sum(src, seg, n):
    return jax.ops.segment_sum(src, seg, n)
kernel_name = 'mk_prb_d1_jaxref_r8_84e0dd'

def setup_inputs(seed: int=0):
    np.random.seed(seed)
    _w = jnp.asarray

    def _L0_attn_setup():
        import jax, jax.numpy as jnp
        import numpy as np
        N_EMBD = 256
        N_Q_HEAD = 16
        N_KV_HEADS = 4
        HEAD_SIZE = N_EMBD // N_Q_HEAD
        GROUP = N_Q_HEAD // N_KV_HEADS
        ROPE_BASE = 10000.0

        def apply_rope(x, seq_offset=0):
            B, H, T, D = x.shape
            half = D // 2
            inv_freq = 1.0 / ROPE_BASE ** (jnp.arange(0, half, dtype=jnp.float32) / half)
            pos = jnp.arange(seq_offset, seq_offset + T, dtype=jnp.float32)
            ang = pos[:, None] * inv_freq[None, :]
            cos = jnp.cos(ang)[None, None].astype(x.dtype)
            sin = jnp.sin(ang)[None, None].astype(x.dtype)
            x1, x2 = (x[..., :half], x[..., half:])
            return jnp.concatenate([x1 * cos - x2 * sin, x2 * cos + x1 * sin], axis=-1)
        key = jax.random.key(seed)
        k0, k1, k2, k3, k4 = jax.random.split(key, 5)
        B, T = (4, 256)
        s = 1.0 / np.sqrt(N_EMBD)
        x = jax.random.normal(k0, (B, T, N_EMBD), dtype=jnp.float32)
        Wq = jax.random.normal(k1, (N_Q_HEAD * HEAD_SIZE, N_EMBD), dtype=jnp.float32) * s
        Wk = jax.random.normal(k2, (N_KV_HEADS * HEAD_SIZE, N_EMBD), dtype=jnp.float32) * s
        Wv = jax.random.normal(k3, (N_KV_HEADS * HEAD_SIZE, N_EMBD), dtype=jnp.float32) * s
        Wp = jax.random.normal(k4, (N_EMBD, N_Q_HEAD * HEAD_SIZE), dtype=jnp.float32) * s
        return {'x': x, 'Wq': Wq, 'Wk': Wk, 'Wv': Wv, 'Wp': Wp}
    _L0_attn_in = _L0_attn_setup()

    def _L0_ffn_setup():
        import jax, jax.numpy as jnp
        import numpy as np
        H = 256
        I = 176
        E = 16
        K = 2
        SI = I * 2

        def _swiglu(gu, inter):
            g, u = (gu[..., :inter], gu[..., inter:])
            return jax.nn.silu(g) * u
        key = jax.random.key(seed)
        ks = jax.random.split(key, 6)
        s = 0.02
        hidden_states = jax.random.normal(ks[0], (1, 128, H), dtype=jnp.float32)
        gate_w = jax.random.normal(ks[1], (E, H), dtype=jnp.float32) * s
        w_gate_up = jax.random.normal(ks[2], (E, H, 2 * I), dtype=jnp.float32) * s
        w_down = jax.random.normal(ks[3], (E, I, H), dtype=jnp.float32) * s
        shared_gate_up = jax.random.normal(ks[4], (H, 2 * SI), dtype=jnp.float32) * s
        shared_down = jax.random.normal(ks[5], (SI, H), dtype=jnp.float32) * s
        return {'hidden_states': hidden_states, 'gate_w': gate_w, 'w_gate_up': w_gate_up, 'w_down': w_down, 'shared_gate_up': shared_gate_up, 'shared_down': shared_down}
    _L0_ffn_in = _L0_ffn_setup()
    _d = {'L0_attn_x': _L0_attn_in['x'], 'L0_attn_Wq': _L0_attn_in['Wq'], 'L0_attn_Wk': _L0_attn_in['Wk'], 'L0_attn_Wv': _L0_attn_in['Wv'], 'L0_attn_Wp': _L0_attn_in['Wp'], 'L0_ffn_gate_w': _L0_ffn_in['gate_w'], 'L0_ffn_w_gate_up': _L0_ffn_in['w_gate_up'], 'L0_ffn_w_down': _L0_ffn_in['w_down'], 'L0_ffn_shared_gate_up': _L0_ffn_in['shared_gate_up'], 'L0_ffn_shared_down': _L0_ffn_in['shared_down']}
    _x0 = _d['L0_attn_x']
    _d['L0_attn_x'] = jax.random.normal(jax.random.fold_in(jax.random.key(seed), 1), (4, 512, 256), dtype=_x0.dtype)
    del _x0
    return _d

def reference(L0_attn_x, L0_attn_Wq, L0_attn_Wk, L0_attn_Wv, L0_attn_Wp, L0_ffn_gate_w, L0_ffn_w_gate_up, L0_ffn_w_down, L0_ffn_shared_gate_up, L0_ffn_shared_down):

    def _L0_attn_ref(x, Wq, Wk, Wv, Wp):
        import jax, jax.numpy as jnp
        import numpy as np
        N_EMBD = 256
        N_Q_HEAD = 16
        N_KV_HEADS = 4
        HEAD_SIZE = N_EMBD // N_Q_HEAD
        GROUP = N_Q_HEAD // N_KV_HEADS
        ROPE_BASE = 10000.0

        def apply_rope(x, seq_offset=0):
            B, H, T, D = x.shape
            half = D // 2
            inv_freq = 1.0 / ROPE_BASE ** (jnp.arange(0, half, dtype=jnp.float32) / half)
            pos = jnp.arange(seq_offset, seq_offset + T, dtype=jnp.float32)
            ang = pos[:, None] * inv_freq[None, :]
            cos = jnp.cos(ang)[None, None].astype(x.dtype)
            sin = jnp.sin(ang)[None, None].astype(x.dtype)
            x1, x2 = (x[..., :half], x[..., half:])
            return jnp.concatenate([x1 * cos - x2 * sin, x2 * cos + x1 * sin], axis=-1)
        B, T, C = x.shape
        Q = (x @ Wq.T).reshape(B, T, N_Q_HEAD, HEAD_SIZE).transpose(0, 2, 1, 3)
        K = (x @ Wk.T).reshape(B, T, N_KV_HEADS, HEAD_SIZE).transpose(0, 2, 1, 3)
        V = (x @ Wv.T).reshape(B, T, N_KV_HEADS, HEAD_SIZE).transpose(0, 2, 1, 3)
        Q = apply_rope(Q, 0)
        K = apply_rope(K, 0)
        Qg = Q.reshape(B, N_KV_HEADS, GROUP, T, HEAD_SIZE)
        scale = 1.0 / jnp.sqrt(jnp.asarray(HEAD_SIZE, dtype=Q.dtype))
        scores = jnp.einsum('bkgtd,bksd->bkgts', Qg, K) * scale
        causal = jnp.tril(jnp.ones((T, T), dtype=bool))
        scores = jnp.where(causal, scores, jnp.finfo(scores.dtype).min)
        attn = jax.nn.softmax(scores, axis=-1)
        out = jnp.einsum('bkgts,bksd->bkgtd', attn, V)
        out = out.reshape(B, N_Q_HEAD, T, HEAD_SIZE).transpose(0, 2, 1, 3).reshape(B, T, N_Q_HEAD * HEAD_SIZE)
        return out @ Wp.T

    def _L0_ffn_ref(hidden_states, gate_w, w_gate_up, w_down, shared_gate_up, shared_down):
        import jax, jax.numpy as jnp
        import numpy as np
        H = 256
        I = 176
        E = 16
        K = 2
        SI = I * 2

        def _swiglu(gu, inter):
            g, u = (gu[..., :inter], gu[..., inter:])
            return jax.nn.silu(g) * u
        orig_shape = hidden_states.shape
        x = hidden_states.reshape(-1, H)
        logits = jnp.einsum('th,eh->te', x, gate_w)
        scores = jax.nn.softmax(logits, axis=-1)
        topk_w, topk_idx = jax.lax.top_k(scores, K)
        combine = jnp.sum(jax.nn.one_hot(topk_idx, E, dtype=x.dtype) * topk_w[..., None], axis=1)
        gu = jnp.einsum('th,ehj->etj', x, w_gate_up)
        h = _swiglu(gu, I)
        y = jnp.einsum('eti,eih,te->th', h, w_down, combine)
        gu_s = x @ shared_gate_up
        y = y + _swiglu(gu_s, SI) @ shared_down
        return y.reshape(orig_shape)
    x = L0_attn_x
    xn = _layernorm(x, axis=-1)
    x = x + _L0_attn_ref(xn, L0_attn_Wq, L0_attn_Wk, L0_attn_Wv, L0_attn_Wp) + _L0_ffn_ref(xn, L0_ffn_gate_w, L0_ffn_w_gate_up, L0_ffn_w_down, L0_ffn_shared_gate_up, L0_ffn_shared_down)
    return x

_drawn_inputs = setup_inputs


def setup_inputs(seed=0):
    import zlib

    import numpy as np

    out = dict(_drawn_inputs(seed))
    spreads = {}
    factors = {'L0_ffn_gate_w': 8.0,
     'L0_ffn_w_gate_up': 8.0,
     'L0_ffn_w_down': 8.0,
     'L0_ffn_shared_gate_up': 2.876,
     'L0_ffn_shared_down': 2.884}
    for name, (base, spread) in spreads.items():
        noise = np.random.default_rng([zlib.crc32(name.encode()), seed]).standard_normal(out[name].shape)
        drawn = base * np.exp(spread * noise) if base else spread * noise
        out[name] = jnp.asarray(drawn.astype(out[name].dtype))
    for name, factor in factors.items():
        out[name] = (out[name] * factor).astype(out[name].dtype)
    return out
```

```python
from contextlib import ExitStack

import numpy as np

import concourse.bass as bass
from concourse import mybir

F32 = mybir.dt.float32
F32R = mybir.dt.float32r
BF16 = mybir.dt.bfloat16
I32 = mybir.dt.int32
U32 = mybir.dt.uint32
ALU = mybir.AluOpType
ACT = mybir.ActivationFunctionType
AX = mybir.AxisListType.X

P = 128
NB, T, D = 4, 512, 256
NT = NB * T // P
NE, NI, NS = 16, 176, 352
HI = NI // 2
NTILE = 2 * NB * T // P + NE - 1
CW = 256 + 64 + 64 + NE
NEG = -3.0e38
EPS = 1e-5
SH = (128, 128, 96)


class Lane:

    def __init__(self, sem):
        self.sem, self.n, self.ops = sem, 0, []

    def do(self, fn, *after):
        self.n += 1
        self.ops.append((after, fn, self.sem, 1))
        return (self.sem, self.n)

    def dma(self, fn, count, *after):
        count.n += 16
        self.ops.append((after, fn, count.sem, 16))
        return (count.sem, count.n)

    def wait(self, *after):
        self.ops.append((after, None, None, 0))

    def issue(self, eng):
        reached = {}
        for after, fn, sem, inc in self.ops:
            for tok in after:
                for s, v in tok if isinstance(tok, list) else [tok]:
                    if reached.get(s.name, 0) < v:
                        eng.wait_ge(s, v)
                        reached[s.name] = v
            if fn is not None:
                fn(eng).then_inc(sem, inc)


class Count:
    def __init__(self, sem):
        self.sem, self.n = sem, 0


def build(nc, a):
    with ExitStack() as ctx:
        def sb(name, shape, dt, where=ctx):
            return where.enter_context(nc.sbuf_tensor("t_" + name, shape, dt))

        def sem(name):
            return ctx.enter_context(nc.semaphore("s_" + name))

        def counts(name, n):
            return [Count(sem(f"{name}{i}")) for i in range(n)]

        pe, dve, act, pool, sp = (Lane(sem(n)) for n in ("pe", "dve", "act", "pool", "sp"))

        xn_d = nc.dram_tensor("xn_d", (NB * T, D), F32).ap()
        y_d = nc.dram_tensor("y_d", (NTILE * P, D), F32).ap()

        ps = ctx.enter_context(nc.psum_tensor("ps", [P, 8, 512], F32))
        free = [[] for _ in range(8)]

        wcat = sb("wcat", [P, 2, CW], F32)
        wp = sb("wp", [P, 2, D], F32)
        wsg = sb("wsg", [P, 2, 2 * NS], F32)
        wsd = sb("wsd", [P, 3, D], F32)
        idf = sb("idf", [P, P], F32)
        idb = sb("idb", [P, P], BF16)
        cmask = sb("cmask", [P, P], BF16)
        tri = sb("tri", [P, P], BF16)
        oneb = sb("oneb", [P, P], BF16)
        cosv = sb("cosv", [P, 4, 16], F32)
        sinv = sb("sinv", [P, 4, 16], F32)
        iota = sb("iota", [P, P], BF16)
        iof = sb("iof", [P, 64], F32)
        tri16 = sb("tri16", [P, NE, NE], F32)
        pcol = sb("pcol", [P, 1], F32)
        xnT = sb("xnT", [P, 2, NB * T], F32)
        vaug = sb("vaug", [P, NT, 4, 32], F32)
        att = sb("att", [P, NT, D], F32)
        stt = sb("stt", [P, NT, 6], F32)
        mv = sb("mv", [P, NT, 2], F32)
        ve = sb("ve", [P, NT], F32)
        sd = sb("sd", [P, NT], F32)
        r0 = sb("r0", [P, NT], F32)
        r1 = sb("r1", [P, NT], F32)
        rs = sb("rs", [P, NT], F32)
        t1 = sb("t1", [P, 2, 20, 16], F32)
        t2 = sb("t2", [P, 2, 20, 16], F32)
        rq = sb("rq", [P, 2, 20, 16], F32)
        lg = sb("lg", [P, NT, NE], F32)
        m8 = sb("m8", [P, NT, 8], F32)
        i8 = sb("i8", [P, NT, 8], U32)
        ef = sb("ef", [P, 2, NT], F32)
        A1 = sb("A1", [P, 2, NT, NE], F32)
        Ab = sb("Ab", [P, NT, NE], BF16)
        lz = sb("lz", [P, NT, NE], F32)
        pe_ = sb("pe_", [P, NT, NE], F32)
        pq = sb("pq", [P, 2, NT, NE], F32)
        zz = sb("zz", [P, NT], F32)
        rz = sb("rz", [P, NT], F32)
        e2 = sb("e2", [P, NT], F32)
        w2 = sb("w2", [P, NT], F32)
        gt = sb("gt", [P, NE, NE], F32)
        ne = sb("ne", [P, NE], F32)
        nt = sb("nt", [P, NE], F32)
        off = sb("off", [P, NE], F32)
        cend = sb("cend", [P, NE], F32)
        posf = sb("posf", [P, 2, NT], F32)
        posu = sb("posu", [P, 2 * NT], U32)
        ph = sb("ph", [P, 2 * NT], U32)
        pl = sb("pl", [P, 2 * NT], U32)
        phf = sb("phf", [P, 2 * NT], F32)
        plf = sb("plf", [P, 2 * NT], F32)
        ohp = sb("ohp", [P, 2, P], BF16)
        oht = sb("oht", [P, 2, 2 * NTILE], BF16)
        gf = sb("gf", [P, NTILE], F32)
        gidx = sb("gidx", [P, NTILE], U32)
        ec = sb("ec", [1, NTILE, NE], F32)
        es = sb("es", [1, NTILE], F32)
        eo = sb("eo", [1, 2, NTILE], I32)
        oT = sb("oT", [P, 2, 512], F32)
        rd = sb("rd", [P, 2, 4, 4], F32)
        mhl = sb("mhl", [P, 2, 4, 8], F32)
        nm = sb("nm", [P, 2, 4, 4], F32)
        mT = sb("mT", [8, 2, 512], F32)

        inner = ExitStack()
        qst = sb("qst", [P, 8, 16, 64], F32R, inner)
        kst = sb("kst", [P, 8, 4, 64], F32R, inner)
        QS = sb("QS", [P, 3, 4, 512], F32R, inner)
        KS = sb("KS", [P, 3, 512], F32R, inner)
        PT = sb("PT", [P, 3, 4, 512], F32, inner)
        sq = sb("sq", [P, 3, P], F32, inner)
        xb = sb("xb", [P, 2, 4, D], F32, inner)
        xn = sb("xn", [P, 2, 4, D], F32, inner)
        inner.close()
        wgu = sb("wgu", [P, NE, 2, 2 * NI], F32)
        wdn = sb("wdn", [HI, NE, 2, D], F32)
        XG = 4
        xg = sb("xg", [P, XG, D], F32)
        xgT = sb("xgT", [P, 2, 2, P], F32)
        sg = sb("sg", [P, 2, NS], F32)
        hh = sb("hh", [P, 2, NS], F32)
        hT = sb("hT", [P, 2, 3, P], F32)
        YR = 3
        yo = sb("yo", [P, YR, D], F32)
        xr = sb("xr", [P, 2, D], F32)
        FR = 4
        yg = sb("yg", [P, FR, 2, D], F32)
        aT = sb("aT", [P, 2, 2, P], F32)
        fo = sb("fo", [P, 2, D], F32)

        c_x = counts("x", 4)
        c_w = Count(sem("w"))
        c_k = Count(sem("k"))
        c_l = Count(sem("l"))
        c_s = Count(sem("s"))
        x_v = a["x"].rearrange("(b i p) d -> b p i d", i=4, p=P)
        ld_x = [None] * 4

        def load_x(b, *after):
            ld_x[b] = sp.dma(lambda e: e.dma_start(xb[:, b % 2, :, :], x_v[b]), c_x[b], *after)

        load_x(0)
        w_ok = sp.dma(lambda e: e.dma_start(wcat[:], a["wcat"].rearrange("(k p) n -> p k n", p=P)), c_w)
        id_ok = sp.dma(lambda e: e.dma_start(idf[:], a["idf"]), c_l)
        load_x(1)
        for t, n in ((cosv, "cosv"), (sinv, "sinv"), (sq, "sq"), (iof, "iof"), (tri16, "tri16"), (pcol, "pcol")):
            k_ok = sp.dma(lambda e, t=t, n=n: e.dma_start(t[:], a[n]), c_k)
        sp.dma(lambda e: e.dma_start(wp[:], a["wpT"].rearrange("(k p) n -> p k n", p=P)), c_s)
        sp.dma(lambda e: e.dma_start(wsg[:], a["wsg"].rearrange("(k p) n -> p k n", p=P)), c_s)
        sp.dma(lambda e: e.dma_start(wsd[:, 0:2, :], a["wsd"][0:256, :].rearrange("(k p) n -> p k n", p=P)), c_s)
        s_ok = sp.dma(lambda e: e.dma_start(wsd[0:96, 2, :], a["wsd"][256:NS, :]), c_s)

        dve.do(lambda e: e.tensor_copy(idb[:], idf[:]), id_ok)
        for n, t in enumerate((cmask, tri, iota)):
            sq_ok = dve.do(lambda e, n=n, t=t: e.tensor_copy(t[:], sq[:, n, :]), k_ok)
        v_one = pool.do(lambda e: e.memset(vaug[:, :, :, 16:32], 1.0))
        b_one = pool.do(lambda e: e.memset(oneb[:], 1.0))
        k_one = [dve.do(lambda e, s=s: e.memset(KS[64:66, s, :].bitcast(F32), 1.0)) for s in range(3)]

        c_xn = counts("xn", NB)
        xn_ok = [None] * NT
        xn_wr = [None] * NB
        xT_ok = [None] * NT
        xn_read = [None] * NB
        q_read = [None] * 16
        k_read = [None] * 16
        rot_free = [None, None]
        qk_ok = [None] * NT
        v_ok = [None] * NT
        lg_ok = [None] * NT
        rq_free = [[], []]

        def norm(b):
            s = slice(4 * b, 4 * b + 4)
            for j in range(4):
                st = dve.do(lambda e, j=j: e.bn_stats(out=stt[:, 4 * b + j, :], in_=xb[:, b % 2, j, :]), ld_x[b])
            for j in range(4):
                ag = dve.do(lambda e, j=j: e.bn_aggr(out=mv[:, 4 * b + j, :], in_=stt[:, 4 * b + j, :]), st)
            v = dve.do(lambda e: e.tensor_scalar(ve[:, s], mv[:, s, 1], EPS, None, ALU.add), ag)
            q = act.do(lambda e: e.activation(sd[:, s], ve[:, s], ACT.Sqrt), v)
            c = dve.do(lambda e: e.reciprocal(r0[:, s], sd[:, s]), q)
            c = dve.do(lambda e: e.tensor_tensor(r1[:, s], r0[:, s], r0[:, s], ALU.mult), c)
            c = dve.do(lambda e: e.tensor_tensor(r1[:, s], r1[:, s], ve[:, s], ALU.mult), c)
            c = dve.do(lambda e: e.tensor_scalar(r1[:, s], r1[:, s], -0.5, 1.5, ALU.mult, ALU.add), c)
            c = dve.do(lambda e: e.tensor_tensor(rs[:, s], r1[:, s], r0[:, s], ALU.mult), c)
            prior = [xn_wr[b - 2], xn_read[b - 2]] if b >= 2 else []
            for j in range(4):
                i = 4 * b + j
                xn_ok[i] = dve.do(lambda e, j=j, i=i: e.tensor_scalar(
                    xn[:, b % 2, j, :], xb[:, b % 2, j, :], mv[:, i, 0:1], rs[:, i:i + 1], ALU.subtract, ALU.mult),
                    c, *prior)
            xn_wr[b] = sp.dma(lambda e: e.dma_start(
                xn_d.rearrange("(b i p) d -> b p i d", i=4, p=P)[b], xn[:, b % 2, :, :]), c_xn[b], xn_ok[4 * b + 3])

        def turn(pair, bank):
            b, j = pair // 2, 2 * (pair % 2)
            for n in range(4):
                last = pe.do(lambda e, n=n: e.transpose(
                    ps[:, bank, n * P:(n + 1) * P],
                    xn[:, b % 2, j + n % 2, (n // 2) * P:(n // 2 + 1) * P], idf[:]),
                    id_ok, xn_ok[2 * pair + 1], free[bank])
            xn_read[b] = last
            c0 = 2 * pair * P
            ok = act.do(lambda e: e.copy(xnT[:, :, c0:c0 + 2 * P],
                                         ps[:, bank, :].rearrange("p (k t) -> p k t", k=2)), last)
            free[bank] = [ok]
            xT_ok[2 * pair] = xT_ok[2 * pair + 1] = ok

        def project(i, bank):
            for k in range(2):
                mm = pe.do(lambda e, k=k: e.matmul(ps[:, bank, 0:CW], xnT[:, k, i * P:(i + 1) * P], wcat[:, k, :],
                                                   start=k == 0, stop=k == 1), w_ok, xT_ok[i], free[bank])
            qk = ps[:, bank, 0:320].rearrange("p (h d) -> p h d", d=16)
            s, z = i % 2, i % 8
            cs = cosv[:, i % 4, :].unsqueeze(1).broadcast_to([P, 20, 16])
            dve.do(lambda e: e.tensor_tensor(t1[:, s], qk, cs, ALU.mult), mm, k_ok, rq_free[s])
            for o in range(2):
                sn = sinv[:, i % 4, 8 * o:8 * o + 8].unsqueeze(1).broadcast_to([P, 20, 8])
                d = dve.do(lambda e, o=o, sn=sn: e.tensor_tensor(
                    t2[:, s, :, 8 * o:8 * o + 8], qk[:, :, 8 - 8 * o:16 - 8 * o], sn, ALU.mult), mm)
            v_ok[i] = act.do(lambda e: e.copy(
                vaug[:, i, :, 0:16], ps[:, bank, 320:384].rearrange("p (h d) -> p h d", d=16)), d)
            lg_ok[i] = act.do(lambda e: e.copy(lg[:, i, :], ps[:, bank, 384:CW]), d)
            free[bank] = [d, lg_ok[i]]
            old = [q_read[4 * (i // 4 - 2) + 3], k_read[4 * (i // 4 - 2) + 3]] if i >= 8 else []
            c = pool.do(lambda e: e.tensor_tensor(rq[:, s], t1[:, s], t2[:, s], ALU.add), d)
            rq_free[s] = [c]
            qq = qst[:, z].rearrange("p h (r d) -> p h r d", d=16)
            q2 = rq[:, s, 0:16, :].unsqueeze(2).broadcast_to([P, 16, 2, 16])
            h1 = pool.do(lambda e: e.tensor_copy(qq[:, :, 0:4:2, :], q2), c, *old)
            kk = kst[:, z].rearrange("p h (r d) -> p h r d", d=16)
            h2 = pool.do(lambda e: e.tensor_copy(
                kk[:, :, 0:4:3, :], rq[:, s, 16:20, :].unsqueeze(2).broadcast_to([P, 4, 2, 16])), c, *old)
            pool.do(lambda e: e.tensor_tensor(qq[:, :, 1:4:2, :], q2, qq[:, :, 0:4:2, :].bitcast(F32),
                                              ALU.subtract), h1)
            qk_ok[i] = pool.do(lambda e: e.tensor_tensor(
                kk[:, :, 1:3, :], rq[:, s, 16:20, :].unsqueeze(2).broadcast_to([P, 4, 2, 16]),
                kk[:, :, 0:1, :].bitcast(F32).broadcast_to([P, 4, 2, 16]), ALU.subtract), h2)

        def batch(b, tb, qb):
            turn(2 * b, tb[0])
            turn(2 * b + 1, tb[1 % len(tb)])
            for j in range(4):
                project(4 * b + j, qb[j % len(qb)])

        c_m = counts("m", 3)
        c_mt = [None] * 16
        st_read = [None] * 16
        pt_free = [[], [], []]
        npt = [0]
        o_ok = [None] * 16
        att_ok = [None] * 16
        ring = [0]
        mT_free = [[], []]

        def prep(u):
            b, g, r = u // 4, u % 4, u % 3
            prior = [st_read[u - 3]] if u >= 3 else []
            dups = []
            for hp in range(2):
                for tb in range(4):
                    z = (4 * b + tb) % 8
                    h = 4 * g + 2 * hp
                    src = qst[:, z, h:h + 2, :].bitcast(F32).rearrange("p h r -> p (h r)")
                    last = pe.do(lambda e, src=src, tb=tb: e.transpose(
                        ps[:, 7, tb * P:(tb + 1) * P], src, idf[:]), qk_ok[4 * b + tb], free[7])
                q_read[u] = last
                c1 = act.do(lambda e, hp=hp: e.copy(QS[0:64, r, 2 * hp, :], ps[0:64, 7, :]), last, *prior)
                c2 = dve.do(lambda e, hp=hp: e.tensor_copy(QS[0:64, r, 2 * hp + 1, :], ps[64:128, 7, :]), last, *prior)
                free[7] = [c1, c2]
                dups += [c1, c2]
                yield
            for tb in range(4):
                z = (4 * b + tb) % 8
                last = pe.do(lambda e, tb=tb, z=z: e.transpose(
                    ps[0:64, 7, tb * P:(tb + 1) * P], kst[:, z, g, :].bitcast(F32), idf[:]), free[7])
            k_read[u] = last
            c1 = act.do(lambda e: e.copy(KS[0:64, r, :], ps[0:64, 7, :]), last, *prior)
            free[7] = [c1]
            dups += [c1]
            yield
            w = u % 2
            for tb in range(4):
                n = (tb + 1) * P
                per = 4 // (tb + 1) if tb < 2 else 1
                for h0 in range(0, 4, per):
                    bank = 4 + ring[0] % 2
                    ring[0] += 1
                    view = ps[:, bank, 0:per * n].rearrange("p (j n) -> p j n", n=n)
                    mk = cmask[:].unsqueeze(1).broadcast_to([P, per, P])
                    pe.do(lambda e, view=view, mk=mk, n=n: e.matmul(
                        view[:, :, n - P:n], idb[:], mk, start=True, stop=True, skip_group_check=True),
                        sq_ok, free[bank])
                    for j in range(per):
                        mm = pe.do(lambda e, j=j, h0=h0, tb=tb, n=n, bank=bank: e.matmul(
                            ps[:, bank, j * n:(j + 1) * n], QS[0:64, r, h0 + j, tb * P:(tb + 1) * P], KS[0:64, r, 0:n],
                            start=False, stop=True, skip_group_check=True), dups)
                    d = dve.do(lambda e, view=view, tb=tb, h0=h0, per=per: e.tensor_reduce(
                        out=nm[:, w, tb, h0:h0 + per], in_=view, axis=AX, op=ALU.max, negate=True), mm)
                    free[bank] = [d]
                    yield
            mr = mhl[:, w].bitcast(F32R)
            c = dve.do(lambda e: e.tensor_copy(mr[:, :, 0:4], nm[:, w]), d)
            c = dve.do(lambda e: e.tensor_tensor(mr[:, :, 4:8], nm[:, w], mhl[:, w, :, 0:4], ALU.subtract), c)
            yield
            for tb in range(4):
                last = pe.do(lambda e, tb=tb: e.transpose(
                    ps[0:8, 7, tb * P:(tb + 1) * P], mhl[:, w, tb, :], idf[:]), c, free[7])
            c = dve.do(lambda e: e.tensor_copy(mT[:, w, :], ps[0:8, 7, :]), last, mT_free[w])
            free[7] = [c]
            for part in range(2):
                c_mt[u] = sp.dma(lambda e, part=part: e.dma_start(
                    QS[64 + part:65 + part, r, :, :].bitcast(F32),
                    mT[4 * part:4 * part + 4, w, :]), c_m[r], c)
            mT_free[w] = [c_mt[u]]
            yield

        def attend(u):
            b, g, r = u // 4, u % 4, u % 3
            units = [(0, 0, 2, 0), (0, 2, 2, 2), (1, 0, 2, 0), (1, 2, 2, 2), (2, 0, 4, 0), (3, 0, 4, 2)]
            chunk, sel, todo = {}, {}, []

            def weigh(sb_):
                n0 = sb_ * P
                cs = chunk[sb_]
                for h in range(4):
                    mm = pe.do(lambda e, h=h: e.matmul(
                        ps[32 * h:32 * h + 32, 6, n0:512], vaug[:, 4 * b + sb_, g, :], PT[:, cs, h, 0:512 - n0],
                        start=sb_ == 0, stop=sb_ == 3), sel[sb_], v_one, v_ok[4 * b + sb_], free[6])
                pt_free[cs] = [mm]
                return mm

            for sb_, h0, nh, bk in units:
                n = 512 - sb_ * P
                if sb_ not in chunk:
                    chunk[sb_], sel[sb_] = npt[0] % 3, []
                    npt[0] += 1
                cs = chunk[sb_]
                width = 512 if nh == 2 else n
                used = free[bk] + free[bk + 1]
                for j in range(nh):
                    col = j * width
                    bank, col = bk + col // 512, col % 512
                    mm = pe.do(lambda e, j=j, bank=bank, col=col, n=n, sb_=sb_, h0=h0: e.matmul(
                        ps[:, bank, col:col + n], KS[0:66, r, sb_ * P:(sb_ + 1) * P],
                        QS[0:66, r, h0 + j, sb_ * P:512], start=True, stop=True),
                        used, c_mt[u], k_one[r])
                if nh == 2:
                    src = ps[:, bk:bk + 2, 0:n]
                else:
                    src = ps[:, bk:bk + 2, :].rearrange("p k n -> p (k n)")[:, 0:4 * n].rearrange(
                        "p (h n) -> p h n", n=n)
                ex = act.do(lambda e, src=src, cs=cs, h0=h0, nh=nh, n=n: e.activation(
                    PT[:, cs, h0:h0 + nh, 0:n], src, ACT.Exp, scale=0.25), mm, pt_free[cs])
                free[bk], free[bk + 1] = [ex], [ex]
                se = pool.do(lambda e, cs=cs, h0=h0, nh=nh: e.affine_select(
                    out=PT[:, cs, h0:h0 + nh, 0:P], in_=PT[:, cs, h0:h0 + nh, 0:P], pattern=[[0, nh], [1, P]],
                    compare_op=ALU.is_ge, fill=0.0, base=0, channel_multiplier=-1), ex)
                sel[sb_] = [se]
                if h0 + nh == 4:
                    todo.append(sb_)
                    if len(todo) > 1:
                        weigh(todo.pop(0))
                yield
            st_read[u] = mm
            while todo:
                last = weigh(todo.pop(0))
                yield
            o_ok[u] = act.do(lambda e: e.copy(oT[:, u % 2, :], ps[:, 6, :]), last)
            free[6] = [o_ok[u]]
            yield

        def settle(u):
            b, g, w = u // 4, u % 4, u % 2
            for tb in range(4):
                last = pe.do(lambda e, tb=tb: e.transpose(
                    ps[:, 7, tb * P:(tb + 1) * P], oT[:, w, tb * P:(tb + 1) * P], idf[:]), o_ok[u], free[7])
            v = ps[:, 7, :].rearrange("p (t h d) -> p t h d", h=4, d=32)
            c = dve.do(lambda e: e.reciprocal(rd[:, w], v[:, :, :, 16]), last)
            c = dve.do(lambda e: e.tensor_tensor(
                att[:, 4 * b:4 * b + 4, 64 * g:64 * g + 64].rearrange("p t (h d) -> p t h d", d=16),
                v[:, :, :, 0:16], rd[:, w].unsqueeze(3).broadcast_to([P, 4, 4, 16]), ALU.mult), c)
            free[7] = [c]
            att_ok[u] = c
            yield

        g_ok = []
        p_ok = []
        e_ok = []
        w_top = []

        def route():
            for i in range(NT):
                c = dve.do(lambda e, i=i: e.max(out=m8[:, i, :], in_=lg[:, i, :]), lg_ok[i])
            for i in range(NT):
                c = dve.do(lambda e, i=i: e.max_index(out=i8[:, i, :], in_max=m8[:, i, :], in_values=lg[:, i, :]), c)
            yield
            c1 = dve.do(lambda e: e.tensor_copy(ef[:, 0, :], i8[:, :, 0]), c)
            c1 = dve.do(lambda e: e.tensor_copy(ef[:, 1, :], i8[:, :, 1]), c)
            io16 = iof[:, 0:NE].unsqueeze(1).broadcast_to([P, NT, NE])
            for s in range(2):
                c = dve.do(lambda e, s=s: e.tensor_tensor(
                    A1[:, s], io16, ef[:, s, :].unsqueeze(2).broadcast_to([P, NT, NE]), ALU.is_equal), c1, k_ok)
            ab = dve.do(lambda e: e.tensor_tensor(Ab[:], A1[:, 0], A1[:, 1], ALU.add), c)
            c = dve.do(lambda e: e.tensor_tensor(
                lz[:], lg[:], m8[:, :, 0:1].broadcast_to([P, NT, NE]), ALU.subtract), c1)
            c3 = dve.do(lambda e: e.tensor_tensor(e2[:], m8[:, :, 1], m8[:, :, 0], ALU.subtract), c)
            x1 = act.do(lambda e: e.activation(lz[:], lz[:], ACT.Exp), c3)
            x2 = act.do(lambda e: e.activation(e2[:], e2[:], ACT.Exp), c3)
            c = dve.do(lambda e: e.tensor_reduce(out=zz[:], in_=lz[:], axis=AX, op=ALU.add), x1)
            c = dve.do(lambda e: e.reciprocal(rz[:], zz[:]), c)
            w_top.append(dve.do(lambda e: e.tensor_tensor(w2[:], e2[:], rz[:], ALU.mult), c, x2))
            yield
            rb, cb = 4 + ring[0] % 2, 4 + (ring[0] + 1) % 2
            ring[0] += 2
            pe.do(lambda e: e.matmul(ps[:, rb, 0:256], tri[:], Ab[:].rearrange("p i e -> p (i e)"),
                                     start=True, stop=True, skip_group_check=True), ab, sq_ok, free[rb])
            for i in range(NT - 1):
                n = NT - 1 - i
                rr = pe.do(lambda e, i=i, n=n: e.matmul(
                    ps[:, rb, 16 * (i + 1):256].rearrange("p (i e) -> p i e", e=NE), oneb[:],
                    Ab[:, i:i + 1, :].broadcast_to([P, n, NE]), start=False, stop=True,
                    skip_group_check=True), b_one)
            for i in range(NT):
                nn = pe.do(lambda e, i=i: e.matmul(ps[:, cb, 0:NE], oneb[:], Ab[:, i, :],
                                                   start=i == 0, stop=i == NT - 1), free[cb])
            c = dve.do(lambda e: e.tensor_copy(ne[:], ps[:, cb, 0:NE]), nn)
            free[cb] = [c]
            c = dve.do(lambda e: e.tensor_tensor(
                gt[:], ne[:].unsqueeze(2).broadcast_to([P, NE, NE]),
                iof[:, 48:64].unsqueeze(1).broadcast_to([P, NE, NE]), ALU.is_gt), c)
            c = dve.do(lambda e: e.tensor_reduce(out=nt[:], in_=gt[:], axis=AX, op=ALU.add), c)
            c = dve.do(lambda e: e.tensor_tensor(
                gt[:], tri16[:], nt[:].unsqueeze(1).broadcast_to([P, NE, NE]), ALU.mult), c)
            c = dve.do(lambda e: e.tensor_reduce(out=off[:], in_=gt[:], axis=AX, op=ALU.add), c)
            co = dve.do(lambda e: e.tensor_tensor(cend[:], off[:], nt[:], ALU.add), c)
            c = dve.do(lambda e: e.scalar_tensor_tensor(
                out=pe_[:], in0=off[:].unsqueeze(1).broadcast_to([P, NT, NE]), scalar=128.0,
                in1=ps[:, rb, 0:256].rearrange("p (i e) -> p i e", e=NE), op0=ALU.mult, op1=ALU.add), rr, c)
            free[rb] = [c]
            for s in range(2):
                c2 = dve.do(lambda e, s=s: e.tensor_tensor(pq[:, s], A1[:, s], pe_[:], ALU.mult), c)
            for s in range(2):
                c = dve.do(lambda e, s=s: e.tensor_reduce(out=posf[:, s, :], in_=pq[:, s], axis=AX, op=ALU.add), c2)
            c = dve.do(lambda e: e.tensor_copy(posu[:], posf[:].rearrange("p s i -> p (s i)")), c)
            p_ok.append(c)
            c1 = dve.do(lambda e: e.tensor_scalar(ph[:], posu[:], 7, None, ALU.logical_shift_right), c)
            c1 = dve.do(lambda e: e.tensor_scalar(pl[:], posu[:], 127, None, ALU.bitwise_and), c)
            c = dve.do(lambda e: e.tensor_copy(phf[:], ph[:]), c1)
            c = dve.do(lambda e: e.tensor_copy(plf[:], pl[:]), c1)
            k = dve.do(lambda e: e.tensor_tensor(
                ec[:], cend[0:1, :].unsqueeze(1).broadcast_to([1, NTILE, NE]),
                iof[0:1, 0:NTILE].unsqueeze(2).broadcast_to([1, NTILE, NE]), ALU.is_le), co)
            k = dve.do(lambda e: e.tensor_reduce(out=es[:], in_=ec[:], axis=AX, op=ALU.add), k)
            k = dve.do(lambda e: e.tensor_scalar(es[:], es[:], float(NE - 1), None, ALU.min), k)
            dve.do(lambda e: e.tensor_scalar(eo[:, 0, :], es[:], float(4 * NI), None, ALU.mult), k)
            e_ok.append(dve.do(lambda e: e.tensor_scalar(eo[:, 1, :], es[:], float(2 * D), None, ALU.mult), k))
            yield
            bank = 4 + ring[0] % 2
            ring[0] += 1
            used = [[], []]
            for n in range(2 * NT):
                i, w = n % NT, n % 2
                dve.do(lambda e, n=n, w=w: e.tensor_scalar(
                    ohp[:, w, :], iota[:], plf[:, n:n + 1], None, ALU.is_equal), c, used[w])
                dve.do(lambda e, n=n, w=w, i=i: e.tensor_scalar(
                    oht[:, w, 0:NTILE], iota[:, 0:NTILE], phf[:, n:n + 1], float(i), ALU.is_equal, ALU.mult))
                d = dve.do(lambda e, n=n, w=w: e.tensor_scalar(
                    oht[:, w, NTILE:], iota[:, 0:NTILE], phf[:, n:n + 1], pcol[:, 0:1], ALU.is_equal, ALU.mult))
                mm = pe.do(lambda e, n=n, w=w: e.matmul(
                    ps[:, bank, 0:2 * NTILE], ohp[:, w, :], oht[:, w, :], start=n == 0, stop=n == 2 * NT - 1,
                    skip_group_check=True), d, free[bank])
                used[w] = [mm]
            c = dve.do(lambda e: e.tensor_copy(gf[:], ps[:, bank, NTILE:2 * NTILE]), mm)
            c = dve.do(lambda e: e.scalar_tensor_tensor(
                out=gf[:], in0=ps[:, bank, 0:NTILE], scalar=128.0, in1=gf[:], op0=ALU.mult, op1=ALU.add), c)
            free[bank] = [c]
            g_ok.append(dve.do(lambda e: e.tensor_copy(gidx[:], gf[:]), c))
            yield

        acc_ok = [None] * NT
        c_xr = counts("xr", 2)
        xr_free = [[], []]
        sh = {}

        def shared_up(i):
            w = i % 2
            ga, gb = 2 * w, 2 * w + 1
            ld = sp.dma(lambda e: e.dma_start(xr[:, w, :], a["x"][i * P:(i + 1) * P, :]), c_xr[w], xr_free[w])
            for half, bank in ((0, ga), (1, gb)):
                for k in range(2):
                    mm = pe.do(lambda e, k=k, half=half, bank=bank: e.matmul(
                        ps[:, bank, 0:NS], xnT[:, k, i * P:(i + 1) * P], wsg[:, k, half * NS:(half + 1) * NS],
                        start=k == 0, stop=k == 1), s_ok, free[bank])
            si = act.do(lambda e: e.activation(sg[:, w, :], ps[:, ga, 0:NS], ACT.Silu), mm)
            mu = dve.do(lambda e: e.tensor_tensor(hh[:, w, :], sg[:, w, :], ps[:, gb, 0:NS], ALU.mult), si)
            free[ga], free[gb] = [si], [mu]
            sh[i] = (mu, ld)

        def shared_turn(i):
            w = i % 2
            mu, ld = sh[i]
            hb = 4 + w
            for k, n in enumerate(SH):
                last = pe.do(lambda e, k=k, n=n: e.transpose(
                    ps[0:n, hb, k * P:(k + 1) * P], hh[:, w, 128 * k:128 * k + n], idf[:]), mu, free[hb])
            c1 = act.do(lambda e: e.copy(hT[:, w, 0:2, :], ps[:, hb, 0:256].rearrange("p (k t) -> p k t", t=P)), last)
            c1 = act.do(lambda e: e.copy(hT[0:96, w, 2, :], ps[0:96, hb, 256:384]), last)
            free[hb] = [c1]
            ab = 6 + w
            for k in range(2):
                last = pe.do(lambda e, k=k: e.transpose(
                    ps[:, ab, k * P:(k + 1) * P], att[:, i, k * P:(k + 1) * P], idf[:]),
                    att_ok[4 * (i // 4) + 3], free[ab])
            c2 = dve.do(lambda e: e.tensor_copy(aT[:, w], ps[:, ab, 0:256].rearrange("p (k t) -> p k t", t=P)), last)
            sh[i] = (c1, c2, ld)

        def shared_down(i):
            w = i % 2
            c1, c2, ld = sh[i]
            ab = 6 + w
            for k in range(2):
                pe.do(lambda e, k=k: e.matmul(ps[:, ab, 256:512], aT[:, w, k, :], wp[:, k, :],
                                              start=k == 0, stop=False), c2)
            for k, n in enumerate(SH):
                mm = pe.do(lambda e, k=k, n=n: e.matmul(
                    ps[:, ab, 256:512], hT[0:n, w, k, :], wsd[0:n, k, :], start=False, stop=k == 2), c1)
            acc_ok[i] = dve.do(lambda e: e.tensor_tensor(att[:, i, :], ps[:, ab, 256:512], xr[:, w, :], ALU.add),
                               mm, ld)
            free[ab] = [acc_ok[i]]
            xr_free[w] = [acc_ok[i]]

        def shared(lo, hi):
            for i in range(lo, hi + 2):
                if lo <= i - 2:
                    shared_down(i - 2)
                if i < hi:
                    shared_up(i)
                if lo <= i - 1 < hi:
                    shared_turn(i - 1)

        c_g = counts("g", XG)
        c_y = counts("y", YR)
        c_we = Count(sem("we"))
        xg_free = [[] for _ in range(XG)]
        gat = [None] * NTILE
        moe = [dict() for _ in range(NTILE)]
        y_wr = [None] * NTILE
        w_exp = []

        def load_experts(*after):
            for e_ in range(NE):
                t = sp.dma(lambda e, e_=e_: e.dma_start(
                    wgu[:, e_], a["wgu"][e_].rearrange("(k p) n -> p k n", p=P)), c_we, *after)
            for e_ in range(NE):
                t = sp.dma(lambda e, e_=e_: e.dma_start(
                    wdn[:, e_], a["wdn"][e_].rearrange("(k p) n -> p k n", p=HI)), c_we, *after)
            w_exp.append(t)

        def gather(n):
            s = n % XG
            gat[n] = pool.dma(lambda e: e.indirect_dma_start(
                out=xg[:, s, :], out_offset=None, in_=xn_d,
                in_offset=bass.IndirectOffsetOnAxis(ap=gidx[:, n:n + 1], axis=0)), c_g[s], g_ok, xn_wr, xg_free[s])

        def moe_in(n):
            w, bank = n % 2, 2 + n % 2
            for k in range(2):
                last = pe.do(lambda e, k=k: e.transpose(
                    ps[:, bank, k * P:(k + 1) * P], xg[:, n % XG, k * P:(k + 1) * P], idf[:]), gat[n], free[bank])
            xg_free[n % XG] = [last]
            c = act.do(lambda e: e.copy(xgT[:, w], ps[:, bank, 0:256].rearrange("p (k t) -> p k t", t=P)), last)
            free[bank] = [c]
            moe[n]["x"] = c

        def moe_up(n):
            w, bank = n % 2, n % 2
            cell = {}

            def first(e):
                cell["v"] = e.value_load(eo[0:1, 0, n:n + 1], min_val=0, max_val=(NE - 1) * 4 * NI)
                return mul(e, 0)

            def mul(e, k):
                r = wgu[:].rearrange("p e k n -> p (e k n)")[:, bass.ds(cell["v"] + k * 2 * NI, 2 * NI)]
                return e.matmul(ps[:, bank, 0:2 * NI], xgT[:, w, k, :], r, start=k == 0, stop=k == 1)

            pe.do(first, e_ok, w_exp, moe[n]["x"], free[bank])
            mm = pe.do(lambda e: mul(e, 1))
            si = act.do(lambda e: e.activation(sg[:, w, 0:NI], ps[:, bank, 0:NI], ACT.Silu), mm)
            mu = dve.do(lambda e: e.tensor_tensor(hh[:, w, 0:NI], sg[:, w, 0:NI], ps[:, bank, NI:2 * NI], ALU.mult), si)
            free[bank] = [mu]
            moe[n]["h"] = mu

        def moe_turn(n):
            w, bank = n % 2, 4 + n % 2
            for k in range(2):
                last = pe.do(lambda e, k=k: e.transpose(
                    ps[0:HI, bank, k * P:(k + 1) * P], hh[:, w, HI * k:HI * k + HI], idf[:]), moe[n]["h"], free[bank])
            c = dve.do(lambda e: e.tensor_copy(
                hT[0:HI, w, 0:2, :], ps[0:HI, bank, 0:256].rearrange("p (k t) -> p k t", t=P)), last)
            free[bank] = [c]
            moe[n]["t"] = c

        def moe_down(n):
            w, bank, s = n % 2, 6 + n % 2, n % YR
            cell = {}

            def first(e):
                cell["v"] = e.value_load(eo[0:1, 1, n:n + 1], min_val=0, max_val=(NE - 1) * 2 * D)
                return mul(e, 0)

            def mul(e, k):
                r = wdn[:].rearrange("p e k n -> p (e k n)")[:, bass.ds(cell["v"] + k * D, D)]
                return e.matmul(ps[:, bank, 0:D], hT[0:HI, w, k, :], r, start=k == 0, stop=k == 1)

            pe.do(first, moe[n]["t"], free[bank])
            mm = pe.do(lambda e: mul(e, 1))
            prior = [y_wr[n - YR]] if n >= YR else []
            c = dve.do(lambda e: e.tensor_copy(yo[:, s, :], ps[:, bank, 0:D]), mm, *prior)
            free[bank] = [c]
            y_wr[n] = sp.dma(lambda e: e.dma_start(y_d[n * P:(n + 1) * P, :], yo[:, s, :]), c_y[s], c)

        def experts():
            for n in range(-1, NTILE + 2):
                if 0 <= n + 1 < NTILE:
                    moe_in(n + 1)
                if 0 <= n - 2:
                    moe_down(n - 2)
                if 0 <= n < NTILE:
                    moe_up(n)
                if 0 <= n - 1 < NTILE:
                    moe_turn(n - 1)

        c_f = counts("f", FR)
        c_o = counts("o", 2)
        yg_free = [[] for _ in range(FR)]
        o_wr = [None] * NT

        def back(i):
            s = i % FR
            y_all = y_wr[NTILE - YR:]
            for q in range(2):
                t = pool.dma(lambda e, q=q: e.indirect_dma_start(
                    out=yg[:, s, q, :], out_offset=None, in_=y_d,
                    in_offset=bass.IndirectOffsetOnAxis(ap=posu[:, q * NT + i:q * NT + i + 1], axis=0)),
                    c_f[s], p_ok, y_all, yg_free[s])
            return t

        def final(i, t):
            s, w = i % FR, i % 2
            c = dve.do(lambda e: e.scalar_tensor_tensor(
                out=att[:, i, :], in0=yg[:, s, 0, :], scalar=rz[:, i:i + 1], in1=att[:, i, :],
                op0=ALU.mult, op1=ALU.add), t, acc_ok[i], w_top)
            prior = [o_wr[i - 2]] if i >= 2 else []
            c = dve.do(lambda e: e.scalar_tensor_tensor(
                out=fo[:, w, :], in0=yg[:, s, 1, :], scalar=w2[:, i:i + 1], in1=att[:, i, :],
                op0=ALU.mult, op1=ALU.add), c, *prior)
            yg_free[s] = [c]
            o_wr[i] = sp.dma(lambda e: e.dma_start(a["out"][i * P:(i + 1) * P, :], fo[:, w, :]), c_o[w], c)

        def mix(*gens):
            gens = list(gens)
            while gens:
                for g in list(gens):
                    if next(g, "end") == "end":
                        gens.remove(g)

        norm(0)
        norm(1)
        batch(0, [7, 6], [4, 5, 0, 1])
        load_x(2, xn_ok[3])
        load_x(3, xn_ok[7])
        batch(1, [7, 6], [2, 3, 4, 5])
        norm(2)
        norm(3)
        mix(prep(0))
        mix(prep(1))
        routing = None
        for u in range(16):
            if u == 4:
                batch(2, [7], [4, 5])
            if u == 8:
                batch(3, [7], [4, 5])
            if u == 10:
                routing = route()
            gens = [attend(u)]
            if u + 2 < 16:
                gens.append(prep(u + 2))
            if u >= 1:
                gens.append(settle(u - 1))
            if u == 10:
                gens.append(routing)
            mix(*gens)
        mix(settle(15))
        over = [st_read[15], q_read[15], k_read[15], *pt_free[0], *pt_free[1], *pt_free[2], xn_wr[3]]
        for lane in (sp, pool, act, dve):
            lane.wait(over)
        load_experts()
        for n in range(XG):
            gather(n)
        HALF = 8
        shared(0, HALF)

        def experts_and_gathers():
            for n in range(-1, NTILE + 2):
                if 0 <= n + 1 < NTILE:
                    moe_in(n + 1)
                    if n + 1 + XG < NTILE:
                        gather(n + 1 + XG)
                if 0 <= n - 2:
                    moe_down(n - 2)
                if 0 <= n < NTILE:
                    moe_up(n)
                if 0 <= n - 1 < NTILE:
                    moe_turn(n - 1)

        experts_and_gathers()
        rows = {}
        for i in range(FR):
            rows[i] = back(i)
        shared(HALF, NT)
        for i in range(NT):
            final(i, rows[i])
            if i + FR < NT:
                rows[i + FR] = back(i + FR)
        sp.wait(o_wr[NT - 1], o_wr[NT - 2])

        block = ctx.enter_context(nc.Block())
        block.sync(lambda e: sp.issue(e))
        block.gpsimd(lambda e: pool.issue(e))
        block.scalar(lambda e: act.issue(e))
        block.vector(lambda e: dve.issue(e))
        block.tensor(lambda e: pe.issue(e))


def constants():
    half = 8
    inv = (np.float32(1.0) / np.float32(10000.0) ** (np.arange(half, dtype=np.float32) / np.float32(half)))
    ang = np.arange(T, dtype=np.float32)[:, None] * inv.astype(np.float32)[None, :]
    cos, sin = np.cos(ang).astype(np.float32), np.sin(ang).astype(np.float32)
    cosv = np.concatenate([cos, cos], 1).reshape(4, P, 16).transpose(1, 0, 2)
    sinv = np.concatenate([-sin, sin], 1).reshape(4, P, 16).transpose(1, 0, 2)
    r = np.arange(P)
    iof = np.concatenate([np.arange(48), np.arange(16) * 128]).astype(np.float32)
    e = np.arange(NE)
    return {
        "idf": np.eye(P, dtype=np.float32),
        "sq": np.stack([np.where(r[None, :] > r[:, None], NEG, 0.0), r[:, None] < r[None, :],
                        np.broadcast_to(r, (P, P))], axis=1).astype(np.float32),
        "iof": np.broadcast_to(iof, (P, 64)).astype(np.float32),
        "tri16": np.broadcast_to((e[None, :] < e[:, None]), (P, NE, NE)).astype(np.float32),
        "pcol": r[:, None].astype(np.float32),
        "cosv": cosv,
        "sinv": sinv,
    }


def kernel(L0_attn_x, L0_attn_Wq, L0_attn_Wk, L0_attn_Wv, L0_attn_Wp, L0_ffn_gate_w, L0_ffn_w_gate_up,
           L0_ffn_w_down, L0_ffn_shared_gate_up, L0_ffn_shared_down):
    import concourse.bacc as bacc
    from concourse.bass_utils import run_bass_kernel_spmd

    f = np.asarray
    arrays = {
        "x": f(L0_attn_x).reshape(NB * T, D),
        "wcat": np.concatenate([f(L0_attn_Wq).T, f(L0_attn_Wk).T, f(L0_attn_Wv).T, f(L0_ffn_gate_w).T], axis=1),
        "wpT": f(L0_attn_Wp).T,
        "wgu": f(L0_ffn_w_gate_up),
        "wdn": f(L0_ffn_w_down),
        "wsg": f(L0_ffn_shared_gate_up),
        "wsd": f(L0_ffn_shared_down),
        **constants(),
    }
    nc = bacc.Bacc("TRN2", target_bir_lowering=False, num_devices=1)
    ins, aps = {}, {}
    for n, v in arrays.items():
        v = np.ascontiguousarray(v)
        ins["in_" + n] = v
        aps[n] = nc.dram_tensor("in_" + n, v.shape, mybir.dt.from_np(v.dtype), kind="ExternalInput").ap()
    aps["out"] = nc.dram_tensor("out_0", (NB * T, D), F32, kind="ExternalOutput").ap()
    build(nc, aps)
    r = run_bass_kernel_spmd(nc, [ins], core_ids=[0])
    return r.results[0]["out_0"].reshape(NB, T, D)
```

```python
from contextlib import ExitStack

import numpy as np

import concourse.bass as bass
from concourse import mybir

F32 = mybir.dt.float32
F32R = mybir.dt.float32r
BF16 = mybir.dt.bfloat16
I32 = mybir.dt.int32
U32 = mybir.dt.uint32
ALU = mybir.AluOpType
ACT = mybir.ActivationFunctionType
AX = mybir.AxisListType.X

P = 128
NB, T, D = 4, 512, 256
NT = NB * T // P
NE, NI, NS = 16, 176, 352
HI = NI // 2
NTILE = 2 * NB * T // P + NE - 1
CW = 256 + 64 + 64 + NE
NEG = -3.0e38
EPS = 1e-5
SH = (128, 128, 96)


class Lane:

    def __init__(self, sem):
        self.sem, self.n, self.ops = sem, 0, []

    def do(self, fn, *after):
        self.n += 1
        self.ops.append((after, fn, self.sem, 1))
        return (self.sem, self.n)

    def dma(self, fn, count, *after):
        count.n += 16
        self.ops.append((after, fn, count.sem, 16))
        return (count.sem, count.n)

    def wait(self, *after):
        self.ops.append((after, None, None, 0))

    def issue(self, eng):
        reached = {}
        for after, fn, sem, inc in self.ops:
            for tok in after:
                for s, v in tok if isinstance(tok, list) else [tok]:
                    if reached.get(s.name, 0) < v:
                        eng.wait_ge(s, v)
                        reached[s.name] = v
            if fn is not None:
                fn(eng).then_inc(sem, inc)


class Count:
    def __init__(self, sem):
        self.sem, self.n = sem, 0


def build(nc, a):
    with ExitStack() as ctx:
        def sb(name, shape, dt, where=ctx):
            return where.enter_context(nc.sbuf_tensor("t_" + name, shape, dt))

        def sem(name):
            return ctx.enter_context(nc.semaphore("s_" + name))

        def counts(name, n):
            return [Count(sem(f"{name}{i}")) for i in range(n)]

        pe, dve, act, pool, sp = (Lane(sem(n)) for n in ("pe", "dve", "act", "pool", "sp"))

        xn_d = nc.dram_tensor("xn_d", (NB * T, D), F32).ap()

        ps = ctx.enter_context(nc.psum_tensor("ps", [P, 8, 512], F32))
        free = [[] for _ in range(8)]

        wcat = sb("wcat", [P, 2, CW], F32)
        wp = sb("wp", [P, 2, D], F32)
        wsg = sb("wsg", [P, 2, 2 * NS], F32)
        wsd = sb("wsd", [P, 3, D], F32)
        idf = sb("idf", [P, P], F32)
        idb = sb("idb", [P, P], BF16)
        idr = sb("idr", [P, P], F32R)
        cmask = sb("cmask", [P, P], BF16)
        tri = sb("tri", [P, P], BF16)
        oneb = sb("oneb", [P, P], BF16)
        cosv = sb("cosv", [P, 4, 16], F32)
        sinv = sb("sinv", [P, 4, 16], F32)
        iota = sb("iota", [P, P], F32)
        iof = sb("iof", [P, 64], F32)
        tri16 = sb("tri16", [P, NE, NE], F32)
        pcol = sb("pcol", [P, 1], F32)
        pcol2 = sb("pcol2", [P, 1], F32)
        xnT = sb("xnT", [P, 2, NB * T], F32)
        vaug = sb("vaug", [P, NT, 4, 32], F32)
        att = sb("att", [P, NT, D], F32)
        stt = sb("stt", [P, NT, 6], F32)
        mv = sb("mv", [P, NT, 2], F32)
        ve = sb("ve", [P, NT], F32)
        sd = sb("sd", [P, NT], F32)
        r0 = sb("r0", [P, NT], F32)
        r1 = sb("r1", [P, NT], F32)
        rs = sb("rs", [P, NT], F32)
        lg = sb("lg", [P, NT, NE], F32)
        m8 = sb("m8", [P, NT, 8], F32)
        i8 = sb("i8", [P, NT, 8], U32)
        ef = sb("ef", [P, 2, NT], F32)
        zz = sb("zz", [P, NT], F32)
        rz = sb("rz", [P, NT], F32)
        e2 = sb("e2", [P, NT], F32)
        ne = sb("ne", [P, NE], F32)
        nt = sb("nt", [P, NE], F32)
        off = sb("off", [P, NE], F32)
        cend = sb("cend", [P, NE], F32)
        phf = sb("phf", [P, 2 * NT], F32)
        plf = sb("plf", [P, 2 * NT], F32)
        tokv = sb("tokv", [P, 2 * NT], F32)
        wv = sb("wv", [P, 2, NT], F32)
        gf = sb("gf", [P, NTILE], F32)
        wpos = sb("wpos", [P, NTILE], F32)
        gidx = sb("gidx", [P, NTILE], U32)
        sidx = sb("sidx", [P, NTILE], U32)
        es = sb("es", [1, NTILE], F32)
        eo = sb("eo", [1, 2, NTILE], I32)
        oT = sb("oT", [P, 2, 512], F32)
        rd = sb("rd", [P, 2, 4, 4], F32)
        mhl = sb("mhl", [P, 2, 4, 8], F32R)
        nm = sb("nm", [P, 2, 4, 4], F32)
        mT = sb("mT", [8, 2, 512], F32)

        rope = ExitStack()
        t1 = sb("t1", [P, 2, 20, 16], F32, rope)
        t2 = sb("t2", [P, 2, 20, 16], F32, rope)
        rq = sb("rq", [P, 2, 20, 16], F32, rope)
        rope.close()
        A1 = sb("A1", [P, 2, NT, NE], F32)
        Ab = sb("Ab", [P, NT, NE], BF16)
        lz = sb("lz", [P, NT, NE], F32)
        pe_ = sb("pe_", [P, NT, NE], F32)
        pq = sb("pq", [P, 2, NT, NE], F32)
        gt = sb("gt", [P, NE, NE], F32)
        ec = sb("ec", [1, NTILE, NE], F32)
        ohp = sb("ohp", [P, 2, P], F32)
        oht = sb("oht", [P, 2, 2 * NTILE], F32)
        ph = sb("ph", [P, 2 * NT], U32)
        pl = sb("pl", [P, 2 * NT], U32)
        posu = sb("posu", [P, 2 * NT], U32)
        posf = sb("posf", [P, 2, NT], F32)
        sg = sb("sg", [P, 2, NS], F32)
        hh = sb("hh", [P, 2, NS], F32)
        hT = sb("hT", [P, 2, 3, P], F32)
        xr = sb("xr", [P, 2, D], F32)
        aT = sb("aT", [P, 2, 2, P], F32)
        fo = sb("fo", [P, 2, D], F32)

        inner = ExitStack()
        qst = sb("qst", [P, 8, 16, 64], F32R, inner)
        kst = sb("kst", [P, 8, 4, 64], F32R, inner)
        QS = sb("QS", [P, 3, 4, 512], F32R, inner)
        KS = sb("KS", [P, 3, 512], F32R, inner)
        PT = sb("PT", [P, 3, 4, 512], F32, inner)
        sq = sb("sq", [P, 3, P], F32, inner)
        xb = sb("xb", [P, 2, 4, D], F32, inner)
        xn = sb("xn", [P, 4, D], F32, inner)
        inner.close()
        wgu = sb("wgu", [P, NE, 2, 2 * NI], F32)
        wdn = sb("wdn", [HI, NE, 2, D], F32)
        XG = 4
        xg = sb("xg", [P, XG, D], F32)
        xgT = sb("xgT", [P, 2, 2, P], F32)
        YR = 3
        yo = sb("yo", [P, YR, D], F32)

        c_x = counts("x", 4)
        c_w = Count(sem("w"))
        c_k = Count(sem("k"))
        c_l = Count(sem("l"))
        c_z = Count(sem("z"))
        c_s = Count(sem("s"))
        x_v = a["x"].rearrange("(b i p) d -> b p i d", i=4, p=P)
        ld_x = [None] * 4

        def load_x(b, *after):
            ld_x[b] = sp.dma(lambda e: e.dma_start(xb[:, b % 2, :, :], x_v[b]), c_x[b], *after)

        load_x(0)
        w_ok = sp.dma(lambda e: e.dma_start(wcat[:], a["wcat"].rearrange("(k p) n -> p k n", p=P)), c_w)
        id_ok = sp.dma(lambda e: e.dma_start(idf[:], a["idf"]), c_l)
        load_x(1)
        for t, n in ((cosv, "cosv"), (sinv, "sinv"), (sq, "sq"), (iof, "iof"), (tri16, "tri16"), (pcol, "pcol"), (pcol2, "pcol2")):
            k_ok = sp.dma(lambda e, t=t, n=n: e.dma_start(t[:], a[n]), c_k)
        sp.dma(lambda e: e.dma_start(wp[:], a["wpT"].rearrange("(k p) n -> p k n", p=P)), c_s)
        sp.dma(lambda e: e.dma_start(wsg[:], a["wsg"].rearrange("(k p) n -> p k n", p=P)), c_s)
        sp.dma(lambda e: e.dma_start(wsd[:, 0:2, :], a["wsd"][0:256, :].rearrange("(k p) n -> p k n", p=P)), c_s)
        s_ok = sp.dma(lambda e: e.dma_start(wsd[0:96, 2, :], a["wsd"][256:NS, :]), c_s)

        dve.do(lambda e: e.tensor_copy(idb[:], idf[:]), id_ok)
        idr_ok = dve.do(lambda e: e.tensor_copy(idr[:], idf[:]), id_ok)
        for n, t in enumerate((cmask, tri, iota)):
            sq_ok = dve.do(lambda e, n=n, t=t: e.tensor_copy(t[:], sq[:, n, :]), k_ok)
        v_one = pool.do(lambda e: e.memset(vaug[:, :, :, 16:32], 1.0))
        b_one = pool.do(lambda e: e.memset(oneb[:], 1.0))
        k_one = [dve.do(lambda e, s=s: e.memset(KS[64:66, s, :].bitcast(F32), 1.0)) for s in range(3)]

        c_xn = counts("xn", NB)
        xn_ok = [None] * NT
        xn_wr = [None] * NB
        xT_ok = [None] * NT
        xn_read = [None] * NB
        q_read = [None] * 16
        k_read = [None] * 16
        rot_free = [None, None]
        qk_ok = [None] * NT
        v_ok = [None] * NT
        lg_ok = [None] * NT
        rq_free = [[], []]

        n_ok = [None] * NB

        def stats(b):
            s = slice(4 * b, 4 * b + 4)
            for j in range(4):
                st = dve.do(lambda e, j=j: e.bn_stats(out=stt[:, 4 * b + j, :], in_=xb[:, b % 2, j, :]), ld_x[b])
            for j in range(4):
                ag = dve.do(lambda e, j=j: e.bn_aggr(out=mv[:, 4 * b + j, :], in_=stt[:, 4 * b + j, :]), st)
            v = dve.do(lambda e: e.tensor_scalar(ve[:, s], mv[:, s, 1], EPS, None, ALU.add), ag)
            q = act.do(lambda e: e.activation(sd[:, s], ve[:, s], ACT.Sqrt), v)
            c = dve.do(lambda e: e.reciprocal(r0[:, s], sd[:, s]), q)
            c = dve.do(lambda e: e.tensor_tensor(r1[:, s], r0[:, s], r0[:, s], ALU.mult), c)
            c = dve.do(lambda e: e.tensor_tensor(r1[:, s], r1[:, s], ve[:, s], ALU.mult), c)
            c = dve.do(lambda e: e.tensor_scalar(r1[:, s], r1[:, s], -0.5, 1.5, ALU.mult, ALU.add), c)
            n_ok[b] = dve.do(lambda e: e.tensor_tensor(rs[:, s], r1[:, s], r0[:, s], ALU.mult), c)

        def norm(b):
            prior = [xn_wr[b - 1], xn_read[b - 1]] if b >= 1 else []
            for j in range(4):
                i = 4 * b + j
                xn_ok[i] = dve.do(lambda e, j=j, i=i: e.tensor_scalar(
                    xn[:, j, :], xb[:, b % 2, j, :], mv[:, i, 0:1], rs[:, i:i + 1], ALU.subtract, ALU.mult),
                    n_ok[b], *prior)
            xn_wr[b] = sp.dma(lambda e: e.dma_start(
                xn_d.rearrange("(b i p) d -> b p i d", i=4, p=P)[b], xn[:]), c_xn[b], xn_ok[4 * b + 3])

        def turn(pair, bank):
            b, j = pair // 2, 2 * (pair % 2)
            for n in range(4):
                last = pe.do(lambda e, n=n: e.transpose(
                    ps[:, bank, n * P:(n + 1) * P],
                    xn[:, j + n % 2, (n // 2) * P:(n // 2 + 1) * P], idf[:]),
                    id_ok, xn_ok[2 * pair + 1], free[bank])
            xn_read[b] = last
            c0 = 2 * pair * P
            ok = act.do(lambda e: e.copy(xnT[:, :, c0:c0 + 2 * P],
                                         ps[:, bank, :].rearrange("p (k t) -> p k t", k=2)), last)
            free[bank] = [ok]
            xT_ok[2 * pair] = xT_ok[2 * pair + 1] = ok

        def project(i, bank):
            for k in range(2):
                mm = pe.do(lambda e, k=k: e.matmul(ps[:, bank, 0:CW], xnT[:, k, i * P:(i + 1) * P], wcat[:, k, :],
                                                   start=k == 0, stop=k == 1), w_ok, xT_ok[i], free[bank])
            qk = ps[:, bank, 0:320].rearrange("p (h d) -> p h d", d=16)
            s, z = i % 2, i % 8
            cs = cosv[:, i % 4, :].unsqueeze(1).broadcast_to([P, 20, 16])
            dve.do(lambda e: e.tensor_tensor(t1[:, s], qk, cs, ALU.mult), mm, k_ok)
            for o in range(2):
                sn = sinv[:, i % 4, 8 * o:8 * o + 8].unsqueeze(1).broadcast_to([P, 20, 8])
                d = dve.do(lambda e, o=o, sn=sn: e.tensor_tensor(
                    t2[:, s, :, 8 * o:8 * o + 8], qk[:, :, 8 - 8 * o:16 - 8 * o], sn, ALU.mult), mm)
            v_ok[i] = act.do(lambda e: e.copy(
                vaug[:, i, :, 0:16], ps[:, bank, 320:384].rearrange("p (h d) -> p h d", d=16)), d)
            lg_ok[i] = act.do(lambda e: e.copy(lg[:, i, :], ps[:, bank, 384:CW]), d)
            free[bank] = [d, lg_ok[i]]
            old = [q_read[4 * (i // 4 - 2) + 3], k_read[4 * (i // 4 - 2) + 3]] if i >= 8 else []
            c = dve.do(lambda e: e.tensor_tensor(rq[:, s], t1[:, s], t2[:, s], ALU.add), d, rq_free[s])
            qq = qst[:, z].rearrange("p h (r d) -> p h r d", d=16)
            q2 = rq[:, s, 0:16, :].unsqueeze(2).broadcast_to([P, 16, 2, 16])
            h1 = act.do(lambda e: e.copy(qq[:, :, 0:4:2, :], q2), c, *old)
            kk = kst[:, z].rearrange("p h (r d) -> p h r d", d=16)
            h2 = act.do(lambda e: e.copy(
                kk[:, :, 0:4:3, :], rq[:, s, 16:20, :].unsqueeze(2).broadcast_to([P, 4, 2, 16])), c, *old)
            pool.do(lambda e: e.tensor_tensor(qq[:, :, 1:4:2, :], q2, qq[:, :, 0:4:2, :].bitcast(F32),
                                              ALU.subtract), h1)
            qk_ok[i] = pool.do(lambda e: e.tensor_tensor(
                kk[:, :, 1:3, :], rq[:, s, 16:20, :].unsqueeze(2).broadcast_to([P, 4, 2, 16]),
                kk[:, :, 0:1, :].bitcast(F32).broadcast_to([P, 4, 2, 16]), ALU.subtract), h2)
            rq_free[s] = [qk_ok[i]]

        def batch(b, tb, qb):
            for p in range(2):
                turn(2 * b + p, tb[p % len(tb)] if tb else take())
                yield 850
            for j in range(4):
                if qb:
                    bank = qb[j % len(qb)]
                else:
                    bank = take()
                project(4 * b + j, bank)
                yield 1350

        c_m = counts("m", 3)
        c_mt = [None] * 16
        st_read = [None] * 16
        pt_free = [[], [], []]
        npt = [0]
        o_ok = [None] * 16
        att_ok = [None] * 16
        ring = [4, 5, 7]

        def take():
            ring.append(ring.pop(0))
            return ring[-1]

        mT_free = [[], []]

        def prep(u):
            b, g, r = u // 4, u % 4, u % 3
            prior = [st_read[u - 3]] if u >= 3 else []
            dups = []
            for hp in range(2):
                bk = take()
                for tb in range(4):
                    z = (4 * b + tb) % 8
                    h = 4 * g + 2 * hp
                    src = qst[:, z, h:h + 2, :].rearrange("p h r -> p (h r)")
                    last = pe.do(lambda e, src=src, tb=tb, bk=bk: e.transpose(
                        ps[:, bk, tb * P:(tb + 1) * P].bitcast(F32R), src, idr[:]), qk_ok[4 * b + tb], idr_ok, free[bk])
                q_read[u] = last
                c1 = act.do(lambda e, hp=hp, bk=bk: e.copy(QS[0:64, r, 2 * hp, :], ps[0:64, bk, :]), last, *prior)
                c2 = dve.do(lambda e, hp=hp, bk=bk: e.tensor_copy(QS[0:64, r, 2 * hp + 1, :], ps[64:128, bk, :]), last, *prior)
                free[bk] = [c1, c2]
                dups += [c1, c2]
                yield 600
            bk = take()
            for tb in range(4):
                z = (4 * b + tb) % 8
                last = pe.do(lambda e, tb=tb, z=z, bk=bk: e.transpose(
                    ps[0:64, bk, tb * P:(tb + 1) * P].bitcast(F32R), kst[:, z, g, :], idr[:]), free[bk])
            k_read[u] = last
            c1 = act.do(lambda e, bk=bk: e.copy(KS[0:64, r, :], ps[0:64, bk, :]), last, *prior)
            free[bk] = [c1]
            dups += [c1]
            yield 800
            w = u % 2
            for tb in range(4):
                n = (tb + 1) * P
                per = 4 // (tb + 1) if tb < 2 else 1
                for h0 in range(0, 4, per):
                    bank = take()
                    view = ps[:, bank, 0:per * n].rearrange("p (j n) -> p j n", n=n)
                    mk = cmask[:].unsqueeze(1).broadcast_to([P, per, P])
                    pe.do(lambda e, view=view, mk=mk, n=n: e.matmul(
                        view[:, :, n - P:n], idb[:], mk, start=True, stop=True, skip_group_check=True),
                        sq_ok, free[bank])
                    for j in range(per):
                        mm = pe.do(lambda e, j=j, h0=h0, tb=tb, n=n, bank=bank: e.matmul(
                            ps[:, bank, j * n:(j + 1) * n], QS[0:64, r, h0 + j, tb * P:(tb + 1) * P], KS[0:64, r, 0:n],
                            start=False, stop=True, skip_group_check=True), dups)
                    d = dve.do(lambda e, view=view, tb=tb, h0=h0, per=per: e.tensor_reduce(
                        out=nm[:, w, tb, h0:h0 + per], in_=view, axis=AX, op=ALU.max, negate=True), mm)
                    free[bank] = [d]
                    yield 600
            mr = mhl[:, w]
            c = dve.do(lambda e: e.tensor_copy(mr[:, :, 0:4], nm[:, w]), d)
            c = dve.do(lambda e: e.tensor_tensor(mr[:, :, 4:8], nm[:, w], mr[:, :, 0:4].bitcast(F32), ALU.subtract), c)
            yield 1500
            bk = take()
            for tb in range(4):
                last = pe.do(lambda e, tb=tb, bk=bk: e.transpose(
                    ps[0:8, bk, tb * P:(tb + 1) * P].bitcast(F32R), mhl[:, w, tb, :], idr[:]), c, free[bk])
            c = dve.do(lambda e, bk=bk: e.tensor_copy(mT[:, w, :], ps[0:8, bk, :]), last, mT_free[w])
            free[bk] = [c]
            for part in range(2):
                c_mt[u] = sp.dma(lambda e, part=part: e.dma_start(
                    QS[64 + part:65 + part, r, :, :].bitcast(F32),
                    mT[4 * part:4 * part + 4, w, :]), c_m[r], c)
            mT_free[w] = [c_mt[u]]
            yield 300

        PREP = 3 * 650 + 11 * 600 + 1800

        sel, chunk = {}, {}
        stb = [0]

        def weigh(u, sb_):
            b, g = u // 4, u % 4
            n0 = sb_ * P
            cs = chunk[u, sb_]
            for h in range(4):
                mm = pe.do(lambda e, h=h: e.matmul(
                    ps[32 * h:32 * h + 32, 6, n0:512], vaug[:, 4 * b + sb_, g, :], PT[:, cs, h, 0:512 - n0],
                    start=sb_ == 0, stop=sb_ == 3), sel[u, sb_], v_one, v_ok[4 * b + sb_], free[6])
            pt_free[cs] = [mm]
            if sb_ == 3:
                o_ok[u] = act.do(lambda e: e.copy(oT[:, u % 2, :], ps[:, 6, :]), mm)
                free[6] = [o_ok[u]]
            return (512 - n0) * 5 // 3 + 80

        def attend(u):
            r = u % 3
            for sb_ in range(4):
                n = 512 - sb_ * P
                chunk[u, sb_] = cs = npt[0] % 3
                npt[0] += 1
                nh = (1, 1, 2, 4)[sb_]
                for h0 in range(0, 4, nh):
                    bk = stb[0] % 2
                    stb[0] += 1
                    for j in range(nh):
                        mm = pe.do(lambda e, j=j, bk=bk, n=n, sb_=sb_, h0=h0: e.matmul(
                            ps[:, bk, j * n:(j + 1) * n], KS[0:66, r, sb_ * P:(sb_ + 1) * P],
                            QS[0:66, r, h0 + j, sb_ * P:512], start=True, stop=True), free[bk], c_mt[u], k_one[r])
                    ex = act.do(lambda e, bk=bk, cs=cs, h0=h0, nh=nh, n=n: e.activation(
                        PT[:, cs, h0:h0 + nh, 0:n], ps[:, bk, 0:nh * n].rearrange("p (h n) -> p h n", n=n),
                        ACT.Exp, scale=0.25), mm, pt_free[cs])
                    free[bk] = [ex]
                    yield 650
                sel[u, sb_] = [pool.do(lambda e, cs=cs: e.affine_select(
                    out=PT[:, cs, :, 0:P], in_=PT[:, cs, :, 0:P], pattern=[[0, 4], [1, P]],
                    compare_op=ALU.is_ge, fill=0.0, base=0, channel_multiplier=-1), ex)]
                if sb_ >= 1:
                    yield weigh(u, sb_ - 1)
                if sb_ == 3:
                    st_read[u] = mm

        ATTEND = 11 * 650 + 2560

        def close(u):
            yield 1500
            yield weigh(u, 3)
            yield 1200
            yield from settle(u)

        def settle(u):
            b, g, w = u // 4, u % 4, u % 2
            bk = take()
            for tb in range(4):
                last = pe.do(lambda e, tb=tb: e.transpose(
                    ps[:, bk, tb * P:(tb + 1) * P], oT[:, w, tb * P:(tb + 1) * P], idf[:]), o_ok[u], free[bk])
            v = ps[:, bk, :].rearrange("p (t h d) -> p t h d", h=4, d=32)
            c = dve.do(lambda e: e.reciprocal(rd[:, w], v[:, :, :, 16]), last)
            c = dve.do(lambda e: e.tensor_tensor(
                att[:, 4 * b:4 * b + 4, 64 * g:64 * g + 64].rearrange("p t (h d) -> p t h d", d=16),
                v[:, :, :, 0:16], rd[:, w].unsqueeze(3).broadcast_to([P, 4, 4, 16]), ALU.mult), c)
            free[bk] = [c]
            att_ok[u] = c
            yield 900

        g_ok = []
        p_ok = []
        e_ok = []

        def route():
            dve.wait(qk_ok[NT - 1], qk_ok[NT - 2])
            for i in range(NT):
                c = dve.do(lambda e, i=i: e.max(out=m8[:, i, :], in_=lg[:, i, :]), lg_ok[i])
            for i in range(NT):
                c = dve.do(lambda e, i=i: e.max_index(out=i8[:, i, :], in_max=m8[:, i, :], in_values=lg[:, i, :]), c)
            yield 2000
            c1 = dve.do(lambda e: e.tensor_copy(ef[:, 0, :], i8[:, :, 0]), c)
            c1 = dve.do(lambda e: e.tensor_copy(ef[:, 1, :], i8[:, :, 1]), c)
            io16 = iof[:, 0:NE].unsqueeze(1).broadcast_to([P, NT, NE])
            for s in range(2):
                c = dve.do(lambda e, s=s: e.tensor_tensor(
                    A1[:, s], io16, ef[:, s, :].unsqueeze(2).broadcast_to([P, NT, NE]), ALU.is_equal), c1, k_ok)
            ab = dve.do(lambda e: e.tensor_tensor(Ab[:], A1[:, 0], A1[:, 1], ALU.add), c)
            c = dve.do(lambda e: e.tensor_tensor(
                lz[:], lg[:], m8[:, :, 0:1].broadcast_to([P, NT, NE]), ALU.subtract), c1)
            c3 = dve.do(lambda e: e.tensor_tensor(e2[:], m8[:, :, 1], m8[:, :, 0], ALU.subtract), c)
            x1 = act.do(lambda e: e.activation(lz[:], lz[:], ACT.Exp), c3)
            x2 = act.do(lambda e: e.activation(e2[:], e2[:], ACT.Exp), c3)
            c = dve.do(lambda e: e.tensor_reduce(out=zz[:], in_=lz[:], axis=AX, op=ALU.add), x1)
            c = dve.do(lambda e: e.reciprocal(rz[:], zz[:]), c)
            dve.do(lambda e: e.tensor_copy(wv[:, 0, :], rz[:]), c)
            w_ok2 = dve.do(lambda e: e.tensor_tensor(wv[:, 1, :], e2[:], rz[:], ALU.mult), c, x2)
            yield 2000
            rb, cb = take(), take()
            pe.do(lambda e: e.matmul(ps[:, rb, 0:256], tri[:], Ab[:].rearrange("p i e -> p (i e)"),
                                     start=True, stop=True, skip_group_check=True), ab, sq_ok, free[rb])
            for i in range(NT - 1):
                n = NT - 1 - i
                rr = pe.do(lambda e, i=i, n=n: e.matmul(
                    ps[:, rb, 16 * (i + 1):256].rearrange("p (i e) -> p i e", e=NE), oneb[:],
                    Ab[:, i:i + 1, :].broadcast_to([P, n, NE]), start=False, stop=True,
                    skip_group_check=True), b_one)
            for i in range(NT):
                nn = pe.do(lambda e, i=i: e.matmul(ps[:, cb, 0:NE], oneb[:], Ab[:, i, :],
                                                   start=i == 0, stop=i == NT - 1), free[cb])
            c = dve.do(lambda e: e.tensor_copy(ne[:], ps[:, cb, 0:NE]), nn)
            free[cb] = [c]
            c = dve.do(lambda e: e.tensor_tensor(
                gt[:], ne[:].unsqueeze(2).broadcast_to([P, NE, NE]),
                iof[:, 48:64].unsqueeze(1).broadcast_to([P, NE, NE]), ALU.is_gt), c)
            c = dve.do(lambda e: e.tensor_reduce(out=nt[:], in_=gt[:], axis=AX, op=ALU.add), c)
            c = dve.do(lambda e: e.tensor_tensor(
                gt[:], tri16[:], nt[:].unsqueeze(1).broadcast_to([P, NE, NE]), ALU.mult), c)
            c = dve.do(lambda e: e.tensor_reduce(out=off[:], in_=gt[:], axis=AX, op=ALU.add), c)
            co = dve.do(lambda e: e.tensor_tensor(cend[:], off[:], nt[:], ALU.add), c)
            c = dve.do(lambda e: e.scalar_tensor_tensor(
                out=pe_[:], in0=off[:].unsqueeze(1).broadcast_to([P, NT, NE]), scalar=128.0,
                in1=ps[:, rb, 0:256].rearrange("p (i e) -> p i e", e=NE), op0=ALU.mult, op1=ALU.add), rr, c)
            free[rb] = [c]
            for s in range(2):
                c2 = dve.do(lambda e, s=s: e.tensor_tensor(pq[:, s], A1[:, s], pe_[:], ALU.mult), c)
            for s in range(2):
                c = dve.do(lambda e, s=s: e.tensor_reduce(out=posf[:, s, :], in_=pq[:, s], axis=AX, op=ALU.add), c2)
            c = dve.do(lambda e: e.tensor_copy(posu[:], posf[:].rearrange("p s i -> p (s i)")), c)
            c1 = dve.do(lambda e: e.tensor_scalar(ph[:], posu[:], 7, None, ALU.logical_shift_right), c)
            c1 = dve.do(lambda e: e.tensor_scalar(pl[:], posu[:], 127, None, ALU.bitwise_and), c)
            c = dve.do(lambda e: e.tensor_copy(phf[:], ph[:]), c1)
            c = dve.do(lambda e: e.tensor_copy(plf[:], pl[:]), c1)
            k = dve.do(lambda e: e.tensor_tensor(
                ec[:], cend[0:1, :].unsqueeze(1).broadcast_to([1, NTILE, NE]),
                iof[0:1, 0:NTILE].unsqueeze(2).broadcast_to([1, NTILE, NE]), ALU.is_le), co)
            k = dve.do(lambda e: e.tensor_reduce(out=es[:], in_=ec[:], axis=AX, op=ALU.add), k)
            k = dve.do(lambda e: e.tensor_scalar(es[:], es[:], float(NE - 1), None, ALU.min), k)
            dve.do(lambda e: e.tensor_scalar(eo[:, 0, :], es[:], float(4 * NI), None, ALU.mult), k)
            e_ok.append(dve.do(lambda e: e.tensor_scalar(eo[:, 1, :], es[:], float(2 * D), None, ALU.mult), k))
            yield 2000
            c = dve.do(lambda e: e.tensor_scalar(tokv[:], plf[:], -1.0, pcol2[:, 0:1], ALU.mult, ALU.add), c)
            c = dve.do(lambda e: e.tensor_tensor(
                tokv[:].rearrange("p (s i) -> p s i", s=2), tokv[:].rearrange("p (s i) -> p s i", s=2),
                iof[:, 48:64].unsqueeze(1).broadcast_to([P, 2, NT]), ALU.add), c)
            used = [[], []]
            wf = wv[:].rearrange("p s i -> p (s i)")
            for n in range(2 * NT):
                if n % 4 == 0:
                    bank = take()
                w = n % 2
                dve.do(lambda e, n=n, w=w: e.tensor_scalar(
                    ohp[:, w, :], iota[:], plf[:, n:n + 1], None, ALU.is_equal), c, sq_ok, used[w])
                dve.do(lambda e, n=n, w=w: e.tensor_scalar(
                    oht[:, w, 0:NTILE], iota[:, 0:NTILE], phf[:, n:n + 1], tokv[:, n:n + 1], ALU.is_equal, ALU.mult))
                d = dve.do(lambda e, n=n, w=w: e.tensor_scalar(
                    oht[:, w, NTILE:], iota[:, 0:NTILE], phf[:, n:n + 1], wf[:, n:n + 1], ALU.is_equal, ALU.mult),
                    w_ok2)
                mm = pe.do(lambda e, n=n, w=w, bank=bank: e.matmul(
                    ps[:, bank, 0:2 * NTILE], ohp[:, w, :], oht[:, w, :], start=n % 4 == 0, stop=n % 4 == 3,
                    skip_group_check=True), d, free[bank])
                used[w] = [mm]
                if n % 4 == 3:
                    if n == 3:
                        g1 = dve.do(lambda e, bank=bank: e.tensor_copy(gf[:], ps[:, bank, 0:NTILE]), mm)
                        g2 = dve.do(lambda e, bank=bank: e.tensor_copy(wpos[:], ps[:, bank, NTILE:2 * NTILE]), mm)
                    else:
                        g1 = dve.do(lambda e, bank=bank: e.tensor_tensor(
                            gf[:], ps[:, bank, 0:NTILE], gf[:], ALU.add), mm, g1)
                        g2 = dve.do(lambda e, bank=bank: e.tensor_tensor(
                            wpos[:], ps[:, bank, NTILE:2 * NTILE], wpos[:], ALU.add), mm, g2)
                    free[bank] = [g2]
                    yield 2400
            c = dve.do(lambda e: e.tensor_scalar(
                gf[:], gf[:], pcol[:, 0:1], float(NB * T), ALU.add, ALU.add), g1, g2)
            p_ok.append(dve.do(lambda e: e.tensor_copy(sidx[:], gf[:]), c))
            c = dve.do(lambda e: e.tensor_scalar(gf[:], gf[:], float(NB * T - 1), None, ALU.min), p_ok[-1])
            g_ok.append(dve.do(lambda e: e.tensor_copy(gidx[:], gf[:]), c))
            yield 600

        c_xr = counts("xr", 2)
        c_o = counts("o", 2)
        xr_free = [[], []]
        hh_free = [[], []]
        hT_free = [[], []]
        aT_free = [[], []]
        o_wr = [None] * NT

        def shared(i, ga, gb, hb, ab, smooth):
            w = i % 2
            ld = sp.dma(lambda e: e.dma_start(xr[:, w, :], a["x"][i * P:(i + 1) * P, :]), c_xr[w], xr_free[w])
            for half, bank in ((0, ga), (1, gb)):
                for k in range(2):
                    mm = pe.do(lambda e, k=k, half=half, bank=bank: e.matmul(
                        ps[:, bank, 0:NS], xnT[:, k, i * P:(i + 1) * P], wsg[:, k, half * NS:(half + 1) * NS],
                        start=k == 0, stop=k == 1), s_ok, free[bank])
                    if k == 1:
                        free[bank] = [mm]
                    yield 590
            if smooth:
                si = act.do(lambda e: e.activation(sg[:, w, :], ps[:, ga, 0:NS], ACT.Tanh, scale=0.5), mm, hh_free[w])
                m1 = dve.do(lambda e: e.scalar_tensor_tensor(
                    out=sg[:, w, :], in0=sg[:, w, :], scalar=1.0, in1=ps[:, ga, 0:NS], op0=ALU.add, op1=ALU.mult), si)
                mu = dve.do(lambda e: e.scalar_tensor_tensor(
                    out=hh[:, w, :], in0=ps[:, gb, 0:NS], scalar=0.5, in1=sg[:, w, :],
                    op0=ALU.mult, op1=ALU.mult), m1, hh_free[w])
            else:
                m1 = si = act.do(lambda e: e.activation(sg[:, w, :], ps[:, ga, 0:NS], ACT.Silu), mm, hh_free[w])
                mu = dve.do(lambda e: e.tensor_tensor(hh[:, w, :], sg[:, w, :], ps[:, gb, 0:NS], ALU.mult),
                            si, hh_free[w])
            free[ga], free[gb] = [m1], [mu]
            yield 2000
            for k, n in enumerate(SH):
                last = pe.do(lambda e, k=k, n=n: e.transpose(
                    ps[0:n, hb, k * P:(k + 1) * P], hh[:, w, 128 * k:128 * k + n], idf[:]), mu, free[hb])
            hh_free[w] = [last]
            c1 = act.do(lambda e: e.copy(hT[:, w, 0:2, :], ps[:, hb, 0:256].rearrange("p (k t) -> p k t", t=P)),
                        last, hT_free[w])
            c1 = act.do(lambda e: e.copy(hT[0:96, w, 2, :], ps[0:96, hb, 256:384]), last)
            free[hb] = [c1]
            yield 700
            for k in range(2):
                last = pe.do(lambda e, k=k: e.transpose(
                    ps[:, ab, k * P:(k + 1) * P], att[:, i, k * P:(k + 1) * P], idf[:]),
                    att_ok[4 * (i // 4) + 3], free[ab])
            c2 = dve.do(lambda e: e.tensor_copy(aT[:, w], ps[:, ab, 0:256].rearrange("p (k t) -> p k t", t=P)),
                        last, aT_free[w])
            yield 1200
            for k, n in enumerate(SH):
                pe.do(lambda e, k=k, n=n: e.matmul(
                    ps[:, ab, 256:512], hT[0:n, w, k, :], wsd[0:n, k, :], start=k == 0, stop=False), c1, c2)
                yield 430
            for k in range(2):
                mm = pe.do(lambda e, k=k: e.matmul(ps[:, ab, 256:512], aT[:, w, k, :], wp[:, k, :],
                                                   start=False, stop=k == 1))
                if k == 0:
                    yield 430
            hT_free[w] = aT_free[w] = [mm]
            prior = [o_wr[i - 2]] if i >= 2 else [z_wr]
            c = dve.do(lambda e: e.tensor_tensor(fo[:, w, :], ps[:, ab, 256:512], xr[:, w, :], ALU.add),
                       mm, ld, *prior)
            free[ab] = [c]
            xr_free[w] = [c]
            o_wr[i] = sp.dma(lambda e: e.dma_start(a["out"][i * P:(i + 1) * P, :], fo[:, w, :]), c_o[w], c)
            yield 430

        SHARED = 4 * 590 + 2000 + 1900 + 5 * 430

        c_g = counts("g", XG)
        c_y = counts("y", YR)
        c_we = Count(sem("we"))
        xg_free = [[] for _ in range(XG)]
        gat = [None] * NTILE
        moe = [dict() for _ in range(NTILE)]
        y_wr = [None] * NTILE
        w_exp = []

        def load_experts(*after):
            for e_ in range(NE):
                t = sp.dma(lambda e, e_=e_: e.dma_start(
                    wgu[:, e_], a["wgu"][e_].rearrange("(k p) n -> p k n", p=P)), c_we, *after)
            for e_ in range(NE):
                t = sp.dma(lambda e, e_=e_: e.dma_start(
                    wdn[:, e_], a["wdn"][e_].rearrange("(k p) n -> p k n", p=HI)), c_we, *after)
            w_exp.append(t)

        def gather(n):
            s = n % XG
            gat[n] = pool.dma(lambda e, n=n: e.indirect_dma_start(
                out=xg[:, s, :], out_offset=None, in_=xn_d,
                in_offset=bass.IndirectOffsetOnAxis(ap=gidx[:, n:n + 1], axis=0)), c_g[s], g_ok, xn_wr, xg_free[s])

        def moe_in(n):
            w, bank = n % 2, 2 + n % 2
            for k in range(2):
                last = pe.do(lambda e, k=k: e.transpose(
                    ps[:, bank, k * P:(k + 1) * P], xg[:, n % XG, k * P:(k + 1) * P], idf[:]), gat[n], free[bank])
            xg_free[n % XG] = [last]
            c = act.do(lambda e: e.copy(xgT[:, w], ps[:, bank, 0:256].rearrange("p (k t) -> p k t", t=P)), last)
            free[bank] = [c]
            moe[n]["x"] = c

        def moe_up(n):
            w, bank = n % 2, n % 2
            cell = {}

            def first(e):
                cell["v"] = e.value_load(eo[0:1, 0, n:n + 1], min_val=0, max_val=(NE - 1) * 4 * NI)
                return mul(e, 0)

            def mul(e, k):
                r = wgu[:].rearrange("p e k n -> p (e k n)")[:, bass.ds(cell["v"] + k * 2 * NI, 2 * NI)]
                return e.matmul(ps[:, bank, 0:2 * NI], xgT[:, w, k, :], r, start=k == 0, stop=k == 1)

            pe.do(first, e_ok, w_exp, moe[n]["x"], free[bank])
            mm = pe.do(lambda e: mul(e, 1))
            si = act.do(lambda e: e.activation(sg[:, w, 0:NI], ps[:, bank, 0:NI], ACT.Silu), mm)
            mu = dve.do(lambda e: e.tensor_tensor(hh[:, w, 0:NI], sg[:, w, 0:NI], ps[:, bank, NI:2 * NI], ALU.mult), si)
            free[bank] = [mu]
            moe[n]["h"] = mu

        def moe_turn(n):
            w, bank = n % 2, 4 + n % 2
            for k in range(2):
                last = pe.do(lambda e, k=k: e.transpose(
                    ps[0:HI, bank, k * P:(k + 1) * P], hh[:, w, HI * k:HI * k + HI], idf[:]), moe[n]["h"], free[bank])
            c = dve.do(lambda e: e.tensor_copy(
                hT[0:HI, w, 0:2, :], ps[0:HI, bank, 0:256].rearrange("p (k t) -> p k t", t=P)), last)
            free[bank] = [c]
            moe[n]["t"] = c

        def moe_down(n):
            w, bank, s = n % 2, 6 + n % 2, n % YR
            cell = {}

            def first(e):
                cell["v"] = e.value_load(eo[0:1, 1, n:n + 1], min_val=0, max_val=(NE - 1) * 2 * D)
                return mul(e, 0)

            def mul(e, k):
                r = wdn[:].rearrange("p e k n -> p (e k n)")[:, bass.ds(cell["v"] + k * D, D)]
                return e.matmul(ps[:, bank, 0:D], hT[0:HI, w, k, :], r, start=k == 0, stop=k == 1)

            pe.do(first, moe[n]["t"], free[bank])
            mm = pe.do(lambda e: mul(e, 1))
            prior = [y_wr[n - YR]] if n >= YR else []
            c = dve.do(lambda e: e.tensor_scalar(
                yo[:, s, :], ps[:, bank, 0:D], wpos[:, n:n + 1], None, ALU.mult), mm, *prior)
            free[bank] = [c]
            moe[n]["y"] = c

        def scatter(n):
            s = n % YR
            before = [y_wr[n - 1]] if n else [z_wr, o_wr[NT - 1], o_wr[NT - 2]]
            y_wr[n] = pool.dma(lambda e: e.indirect_dma_start(
                out=a["out"], out_offset=bass.IndirectOffsetOnAxis(ap=sidx[:, n:n + 1], axis=0),
                in_=yo[:, s, :], in_offset=None, compute_op=ALU.add), c_y[s], p_ok, moe[n]["y"], before)

        def mix(*items):
            live = [[g, max(total, 1), 0] for g, total in items]
            while live:
                it = min(live, key=lambda it: it[2] / it[1])
                c = next(it[0], None)
                if c is None:
                    live.remove(it)
                else:
                    it[2] += c

        def part(g, budget):
            spent = 0
            while spent < budget:
                c = next(g, None)
                if c is None:
                    return
                spent += c
                yield c

        def chain(*gens):
            for g in gens:
                yield from g

        zero_ok = pool.do(lambda e: e.memset(fo[:, 0, :], 0.0))
        z_wr = sp.dma(lambda e: e.dma_start(a["out"][NB * T:NB * T + P, :], fo[:, 0, :]), c_z, zero_ok)
        stats(0)
        norm(0)
        load_x(2, xn_ok[3])
        first = batch(0, [7, 6], [4, 5, 0, 1])
        mix((part(first, 1700), 1))
        stats(1)
        norm(1)
        load_x(3, xn_ok[7])
        mix((first, 1))
        mix((batch(1, [7, 6], [2, 3, 0, 1]), 7100), (prep(0), PREP))
        stats(2)
        stats(3)
        mix((prep(1), 1))
        qkv = {2: batch(2, None, None), 3: batch(3, None, None)}
        routing = route()
        EARLY = 9
        early = chain(*[shared(i, 2, 3, 2, 3, True) for i in range(EARLY)])
        for u in range(16):
            items = [(attend(u), ATTEND)]
            if u >= 1:
                items.append((close(u - 1), 4100))
            if u + 2 < 16:
                items.append((prep(u + 2), PREP))
            if u in (2, 6):
                norm(2 + u // 6)
            if 2 <= u < 10:
                g = qkv[2 + (u - 2) // 4]
                budget = 1e9 if u in (5, 9) else 1850
                items.append((part(g, budget), 1850))
            if u >= 10:
                items.append((part(routing, 1e9 if u == 15 else 5200), 5200))
            if u >= 5:
                budget = 1e9 if u == 15 else EARLY * SHARED / 11
                items.append((part(early, budget), EARLY * SHARED / 11))
            mix(*items)
        mix((close(15), 1))
        over = [st_read[15], q_read[15], k_read[15], *pt_free[0], *pt_free[1], *pt_free[2], xn_wr[3]]
        for lane in (sp, pool, act, dve):
            lane.wait(over)
        load_experts()
        for n in range(XG):
            gather(n)
        late = [shared(i, 2 * (i % 2), 2 * (i % 2) + 1, 4 + i % 2, 6 + i % 2, False) for i in range(EARLY, NT)]
        lanes = [chain(*late[0::2]), chain(part(iter([SHARED / 2]), 1e9), *late[1::2])]
        mix((lanes[0], 1), (lanes[1], 1))
        moe_in(0)
        moe_in(1)
        for n in range(NTILE + 1):
            if n >= 1:
                moe_turn(n - 1)
            if n < NTILE:
                moe_up(n)
            if n >= 1:
                moe_down(n - 1)
                scatter(n - 1)
            if n + 2 < NTILE:
                moe_in(n + 2)
                if n + XG < NTILE:
                    gather(n + XG)
        sp.wait(y_wr[NTILE - 1])

        block = ctx.enter_context(nc.Block())
        block.sync(lambda e: sp.issue(e))
        block.gpsimd(lambda e: pool.issue(e))
        block.scalar(lambda e: act.issue(e))
        block.vector(lambda e: dve.issue(e))
        block.tensor(lambda e: pe.issue(e))


def constants():
    half = 8
    inv = (np.float32(1.0) / np.float32(10000.0) ** (np.arange(half, dtype=np.float32) / np.float32(half)))
    ang = np.arange(T, dtype=np.float32)[:, None] * inv.astype(np.float32)[None, :]
    cos, sin = np.cos(ang).astype(np.float32), np.sin(ang).astype(np.float32)
    cosv = np.concatenate([cos, cos], 1).reshape(4, P, 16).transpose(1, 0, 2)
    sinv = np.concatenate([-sin, sin], 1).reshape(4, P, 16).transpose(1, 0, 2)
    r = np.arange(P)
    iof = np.concatenate([np.arange(48), np.arange(16) * 128]).astype(np.float32)
    e = np.arange(NE)
    return {
        "idf": np.eye(P, dtype=np.float32),
        "sq": np.stack([np.where(r[None, :] > r[:, None], NEG, 0.0), r[:, None] < r[None, :],
                        np.broadcast_to(r, (P, P))], axis=1).astype(np.float32),
        "iof": np.broadcast_to(iof, (P, 64)).astype(np.float32),
        "tri16": np.broadcast_to((e[None, :] < e[:, None]), (P, NE, NE)).astype(np.float32),
        "pcol": r[:, None].astype(np.float32),
        "pcol2": (r[:, None] - NB * T).astype(np.float32),
        "cosv": cosv,
        "sinv": sinv,
    }


def kernel(L0_attn_x, L0_attn_Wq, L0_attn_Wk, L0_attn_Wv, L0_attn_Wp, L0_ffn_gate_w, L0_ffn_w_gate_up,
           L0_ffn_w_down, L0_ffn_shared_gate_up, L0_ffn_shared_down):
    import concourse.bacc as bacc
    from concourse.bass_utils import run_bass_kernel_spmd

    f = np.asarray
    arrays = {
        "x": f(L0_attn_x).reshape(NB * T, D),
        "wcat": np.concatenate([f(L0_attn_Wq).T, f(L0_attn_Wk).T, f(L0_attn_Wv).T, f(L0_ffn_gate_w).T], axis=1),
        "wpT": f(L0_attn_Wp).T,
        "wgu": f(L0_ffn_w_gate_up),
        "wdn": f(L0_ffn_w_down),
        "wsg": f(L0_ffn_shared_gate_up),
        "wsd": f(L0_ffn_shared_down),
        **constants(),
    }
    nc = bacc.Bacc("TRN2", target_bir_lowering=False, num_devices=1)
    ins, aps = {}, {}
    for n, v in arrays.items():
        v = np.ascontiguousarray(v)
        ins["in_" + n] = v
        aps[n] = nc.dram_tensor("in_" + n, v.shape, mybir.dt.from_np(v.dtype), kind="ExternalInput").ap()
    aps["out"] = nc.dram_tensor("out_0", (NB * T + P, D), F32, kind="ExternalOutput").ap()
    build(nc, aps)
    r = run_bass_kernel_spmd(nc, [ins], core_ids=[0])
    return r.results[0]["out_0"][:NB * T].reshape(NB, T, D)
```

```python
from contextlib import ExitStack

import numpy as np

import concourse.bass as bass
from concourse import mybir

F32 = mybir.dt.float32
F32R = mybir.dt.float32r
BF16 = mybir.dt.bfloat16
I32 = mybir.dt.int32
U32 = mybir.dt.uint32
ALU = mybir.AluOpType
ACT = mybir.ActivationFunctionType
AX = mybir.AxisListType.X

P = 128
NB, T, D = 4, 512, 256
NT = NB * T // P
NE, NI, NS = 16, 176, 352
HI = NI // 2
NTILE = 2 * NB * T // P + NE - 1
CW = 256 + 64 + 64 + NE
NEG = -3.0e38
YR = 4
EPS = 1e-5
SH = (128, 128, 96)


WHEN = {}
LAT = 230


def ready(*after):
    t = 0
    for tok in after:
        if isinstance(tok, list):
            t = max(t, ready(*tok))
        else:
            t = max(t, WHEN[tok[0].name, tok[1]])
    return t


class Lane:

    def __init__(self, sem):
        self.sem, self.n, self.ops, self.t = sem, 0, [], 0

    def do(self, fn, *after, ns=100):
        self.n += 1
        self.ops.append((after, fn, self.sem, 1))
        self.t = max(self.t, ready(*after)) + ns
        WHEN[self.sem.name, self.n] = self.t + LAT
        return (self.sem, self.n)

    def dma(self, fn, count, *after, ns=60, lat=2300):
        count.n += 16
        self.ops.append((after, fn, count.sem, 16))
        self.t = max(self.t, ready(*after)) + ns
        WHEN[count.sem.name, count.n] = self.t + lat
        return (count.sem, count.n)

    def wait(self, *after):
        self.ops.append((after, None, None, 0))

    def issue(self, eng):
        reached = {}
        for after, fn, sem, inc in self.ops:
            for tok in after:
                for s, v in tok if isinstance(tok, list) else [tok]:
                    if reached.get(s.name, 0) < v:
                        eng.wait_ge(s, v)
                        reached[s.name] = v
            if fn is not None:
                fn(eng).then_inc(sem, inc)


class Count:
    def __init__(self, sem):
        self.sem, self.n = sem, 0


def build(nc, a):
    WHEN.clear()
    with ExitStack() as ctx:
        def sb(name, shape, dt, where=ctx):
            return where.enter_context(nc.sbuf_tensor("t_" + name, shape, dt))

        def sem(name):
            return ctx.enter_context(nc.semaphore("s_" + name))

        def counts(name, n):
            return [Count(sem(f"{name}{i}")) for i in range(n)]

        pe, dve, act, pool, sp = (Lane(sem(n)) for n in ("pe", "dve", "act", "pool", "sp"))

        xn_d = nc.dram_tensor("xn_d", (NB * T, D), F32).ap()

        ps = ctx.enter_context(nc.psum_tensor("ps", [P, 8, 512], F32))
        free = [[] for _ in range(8)]

        wcat = sb("wcat", [P, 2, CW], F32)
        wp = sb("wp", [P, 2, D], F32)
        wsg = sb("wsg", [P, 2, 2 * NS], F32)
        wsd = sb("wsd", [P, 3, D], F32)
        idf = sb("idf", [P, P], F32)
        idb = sb("idb", [P, P], BF16)
        idr = sb("idr", [P, P], F32R)
        cmask = sb("cmask", [P, P], BF16)
        tri = sb("tri", [P, P], BF16)
        oneb = sb("oneb", [P, P], BF16)
        cosv = sb("cosv", [P, 4, 16], F32)
        sinv = sb("sinv", [P, 4, 16], F32)
        iota = sb("iota", [P, P], F32)
        iof = sb("iof", [P, 64], F32)
        tri16 = sb("tri16", [P, NE, NE], F32)
        posc = sb("posc", [P, NTILE], F32)
        tokc = sb("tokc", [P, 2 * NT], F32)
        xnT = sb("xnT", [P, 2, NB * T], F32)
        vaug = sb("vaug", [P, NT, 4, 32], F32)
        att = sb("att", [P, NT, D], F32)
        stt = sb("stt", [P, NT, 6], F32)
        mv = sb("mv", [P, NT, 2], F32)
        ve = sb("ve", [P, NT], F32)
        sd = sb("sd", [P, NT], F32)
        r0 = sb("r0", [P, NT], F32)
        r1 = sb("r1", [P, NT], F32)
        rs = sb("rs", [P, NT], F32)
        lg = sb("lg", [P, NT, NE], F32)
        m8 = sb("m8", [P, NT, 8], F32)
        i8 = sb("i8", [P, NT, 8], U32)
        ef = sb("ef", [P, 2, NT], F32)
        zz = sb("zz", [P, NT], F32)
        rz = sb("rz", [P, NT], F32)
        e2 = sb("e2", [P, NT], F32)
        ne = sb("ne", [P, NE], F32)
        nt = sb("nt", [P, NE], F32)
        off = sb("off", [P, NE], F32)
        cend = sb("cend", [P, NE], F32)
        phf = sb("phf", [P, 2 * NT], F32)
        plf = sb("plf", [P, 2 * NT], F32)
        tokv = sb("tokv", [P, 2 * NT], F32)
        wv = sb("wv", [P, 2, NT], F32)
        gw = sb("gw", [P, 2 * NTILE], F32)
        gidx = sb("gidx", [P, NTILE], U32)
        sidx = sb("sidx", [P, NTILE], U32)
        es = sb("es", [1, NTILE], F32)
        eo = sb("eo", [1, 2, NTILE], I32)
        oT = sb("oT", [P, 2, 512], F32)
        rd = sb("rd", [P, 2, 4, 4], F32)
        mhl = sb("mhl", [P, 2, 4, 8], F32R)
        nm = sb("nm", [P, 2, 4, 4], F32)
        mT = sb("mT", [8, 2, 512], F32)

        rope = ExitStack()
        t1 = sb("t1", [P, 2, 20, 16], F32, rope)
        t2 = sb("t2", [P, 2, 20, 16], F32, rope)
        rq = sb("rq", [P, 2, 20, 16], F32, rope)
        rope.close()
        A1 = sb("A1", [P, 2, NT, NE], F32)
        Ab = sb("Ab", [P, NT, NE], BF16)
        lz = sb("lz", [P, NT, NE], F32)
        pe_ = sb("pe_", [P, NT, NE], F32)
        pq = sb("pq", [P, 2, NT, NE], F32)
        gt = sb("gt", [P, NE, NE], F32)
        early = ExitStack()
        ec = sb("ec", [1, NTILE, NE], F32, early)
        early.close()
        ohp = sb("ohp", [P, 4, P], F32)
        oht = sb("oht", [P, 4, 2 * NTILE], F32)
        ph = sb("ph", [P, 2 * NT], U32)
        pl = sb("pl", [P, 2 * NT], U32)
        posu = sb("posu", [P, 2 * NT], U32)
        posf = sb("posf", [P, 2, NT], F32)
        sg = sb("sg", [P, 2, NS], F32)
        hh = sb("hh", [P, 2, NS], F32)
        hT = sb("hT", [P, 2, 3, P], F32)
        xr = sb("xr", [P, 2, D], F32)
        aT = sb("aT", [P, 2, 2, P], F32)
        fo = sb("fo", [P, 2, D], F32)

        inner = ExitStack()
        qst = sb("qst", [P, 8, 16, 64], F32R, inner)
        kst = sb("kst", [P, 8, 4, 64], F32R, inner)
        xb = sb("xb", [P, 2, 4, D], F32, inner)
        xn = sb("xn", [P, 4, D], F32, inner)
        sq = sb("sq", [P, 3, P], F32, inner)
        QS = sb("QS", [P, 3, 4, 512], F32R, inner)
        KS = sb("KS", [P, 3, 512], F32R, inner)
        PT = sb("PT", [P, 3, 4, 512], F32, inner)
        inner.close()
        wgu = sb("wgu", [P, NE, 2, 2 * NI], F32)
        wdn = sb("wdn", [HI, NE, 2, D], F32)
        XG = 4
        xg = sb("xg", [P, XG, D], F32)
        xgT = sb("xgT", [P, 2, 2, P], F32)
        yo = sb("yo", [P, YR, D], F32)

        c_x = counts("x", 4)
        c_t = Count(sem("t"))
        c_w = Count(sem("w"))
        c_k = Count(sem("k"))
        c_l = Count(sem("l"))
        c_z = Count(sem("z"))
        c_s = Count(sem("s"))
        x_v = a["x"].rearrange("(b i p) d -> b p i d", i=4, p=P)
        ld_x = [None] * 4

        def load_x(b, *after):
            ld_x[b] = sp.dma(lambda e: e.dma_start(xb[:, b % 2, :, :], x_v[b]), c_x[b], *after)

        load_x(0)
        w_ok = sp.dma(lambda e: e.dma_start(wcat[:], a["wcat"].rearrange("(k p) n -> p k n", p=P)), c_w)
        id_ok = sp.dma(lambda e: e.dma_start(idf[:], a["idf"]), c_l)
        for t, n in ((cosv, "cosv"), (sinv, "sinv"), (sq, "sq"), (iof, "iof"), (tri16, "tri16"), (posc, "posc"), (tokc, "tokc")):
            k_ok = sp.dma(lambda e, t=t, n=n: e.dma_start(t[:], a[n]), c_k)
        load_x(1)
        xt = PT[:, 2].rearrange("p h n -> p (h n)").rearrange("p (b i d) -> p b i d", b=2, d=D)
        for b in (2, 3):
            ld_t = sp.dma(lambda e, b=b: e.dma_start(xt[:, b - 2], x_v[b]), c_t)
        sp.dma(lambda e: e.dma_start(wp[:], a["wpT"].rearrange("(k p) n -> p k n", p=P)), c_s)
        sp.dma(lambda e: e.dma_start(wsg[:], a["wsg"].rearrange("(k p) n -> p k n", p=P)), c_s)
        sp.dma(lambda e: e.dma_start(wsd[:, 0:2, :], a["wsd"][0:256, :].rearrange("(k p) n -> p k n", p=P)), c_s)
        s_ok = sp.dma(lambda e: e.dma_start(wsd[0:96, 2, :], a["wsd"][256:NS, :]), c_s)

        dve.do(lambda e: e.tensor_copy(idb[:], idf[:]), id_ok)
        idr_ok = dve.do(lambda e: e.tensor_copy(idr[:], idf[:]), id_ok)
        v_one = pool.do(lambda e: e.memset(vaug[:, :, :, 16:32], 1.0))
        b_one = pool.do(lambda e: e.memset(oneb[:], 1.0))
        sq_ok = []

        ring = [0, 1, 4, 5, 7]

        def take(bank=None):
            return bank if bank is not None else min(ring, key=lambda k: ready(free[k]))

        def at(after, bank=None):
            return lambda: max(ready(*after), ready(free[bank]) if bank is not None else
                               min(ready(free[k]) for k in ring))

        def blocked(cond, then):
            return lambda: None if cond() else then()

        def order(chains, *until):
            live = [c if isinstance(c, list) else [c, next(c, "end")] for c in chains]
            need = [c for c, u in zip(live, until) if u]
            while any(c[1] != "end" for c in need):
                best = None
                for c in live:
                    t = None if c[1] == "end" else c[1]()
                    if t is not None:
                        t = max(t, pe.t + 80)
                        if best is None or t < best[0]:
                            best = (t, c)
                best[1][1] = next(best[1][0], "end")
            return live

        c_xn = counts("xn", NB)
        xn_ok = [None] * NT
        xn_wr = [None] * NB
        xT_ok = [None] * NT
        xn_read = [None] * NB
        q_read = [None] * 16
        k_read = [None] * 16
        rot_free = [None, None]
        qk_ok = [None] * NT
        v_ok = [None] * NT
        lg_ok = [None] * NT
        rq_free = [[], []]

        n_ok = [None] * NB

        def x_in(b, j):
            return xb[:, b, j, :] if b < 2 else xt[:, b - 2, j, :]

        def stats(b):
            s = slice(4 * b, 4 * b + 4)
            for j in range(4):
                st = dve.do(lambda e, j=j: e.bn_stats(out=stt[:, 4 * b + j, :], in_=x_in(b, j)), ld_x[b] if b < 2 else ld_t)
            for j in range(4):
                ag = dve.do(lambda e, j=j: e.bn_aggr(out=mv[:, 4 * b + j, :], in_=stt[:, 4 * b + j, :]), st)
            v = dve.do(lambda e: e.tensor_scalar(ve[:, s], mv[:, s, 1], EPS, None, ALU.add), ag)
            q = act.do(lambda e: e.activation(sd[:, s], ve[:, s], ACT.Sqrt), v)
            c = dve.do(lambda e: e.reciprocal(r0[:, s], sd[:, s]), q)
            c = dve.do(lambda e: e.tensor_tensor(r1[:, s], r0[:, s], r0[:, s], ALU.mult), c)
            c = dve.do(lambda e: e.tensor_tensor(r1[:, s], r1[:, s], ve[:, s], ALU.mult), c)
            c = dve.do(lambda e: e.tensor_scalar(r1[:, s], r1[:, s], -0.5, 1.5, ALU.mult, ALU.add), c)
            n_ok[b] = dve.do(lambda e: e.tensor_tensor(rs[:, s], r1[:, s], r0[:, s], ALU.mult), c)

        def norm(b):
            prior = [xn_wr[b - 1], xn_read[b - 1]] if b >= 1 else []
            for j in range(4):
                i = 4 * b + j
                xn_ok[i] = dve.do(lambda e, j=j, i=i: e.tensor_scalar(
                    xn[:, j, :], xb[:, b % 2, j, :], mv[:, i, 0:1], rs[:, i:i + 1], ALU.subtract, ALU.mult),
                    n_ok[b], ld_x[b], *prior, ns=323)
            xn_wr[b] = sp.dma(lambda e: e.dma_start(
                xn_d.rearrange("(b i p) d -> b p i d", i=4, p=P)[b], xn[:]), c_xn[b], xn_ok[4 * b + 3])

        def turn(pair, bank):
            b, j = pair // 2, 2 * (pair % 2)
            for n in range(4):
                last = pe.do(lambda e, n=n: e.transpose(
                    ps[:, bank, n * P:(n + 1) * P],
                    xn[:, j + n % 2, (n // 2) * P:(n // 2 + 1) * P], idf[:]),
                    id_ok, xn_ok[2 * pair + 1], free[bank], ns=107)
            xn_read[b] = last
            c0 = 2 * pair * P
            ok = act.do(lambda e: e.copy(xnT[:, :, c0:c0 + 2 * P],
                                         ps[:, bank, :].rearrange("p (k t) -> p k t", k=2)), last, ns=478)
            free[bank] = [ok]
            xT_ok[2 * pair] = xT_ok[2 * pair + 1] = ok

        def project(i, bank):
            for k in range(2):
                mm = pe.do(lambda e, k=k: e.matmul(ps[:, bank, 0:CW], xnT[:, k, i * P:(i + 1) * P], wcat[:, k, :],
                                                   start=k == 0, stop=k == 1), w_ok, xT_ok[i], free[bank], ns=667)
            qk = ps[:, bank, 0:320].rearrange("p (h d) -> p h d", d=16)
            s, z = i % 2, i % 8
            cs = cosv[:, i % 4, :].unsqueeze(1).broadcast_to([P, 20, 16])
            dve.do(lambda e: e.tensor_tensor(t1[:, s], qk, cs, ALU.mult), mm, k_ok, ns=402)
            for o in range(2):
                sn = sinv[:, i % 4, 8 * o:8 * o + 8].unsqueeze(1).broadcast_to([P, 20, 8])
                d = dve.do(lambda e, o=o, sn=sn: e.tensor_tensor(
                    t2[:, s, :, 8 * o:8 * o + 8], qk[:, :, 8 - 8 * o:16 - 8 * o], sn, ALU.mult), mm, ns=235)
            v_ok[i] = act.do(lambda e: e.copy(
                vaug[:, i, :, 0:16], ps[:, bank, 320:384].rearrange("p (h d) -> p h d", d=16)), d)
            lg_ok[i] = act.do(lambda e: e.copy(lg[:, i, :], ps[:, bank, 384:CW]), d)
            free[bank] = [d, lg_ok[i]]
            old = [q_read[4 * (i // 4 - 2) + 3], k_read[4 * (i // 4 - 2) + 3]] if i >= 8 else []
            c = dve.do(lambda e: e.tensor_tensor(rq[:, s], t1[:, s], t2[:, s], ALU.add), d, rq_free[s], ns=402)
            qq = qst[:, z].rearrange("p h (r d) -> p h r d", d=16)
            q2 = rq[:, s, 0:16, :].unsqueeze(2).broadcast_to([P, 16, 2, 16])
            h1 = act.do(lambda e: e.copy(qq[:, :, 0:4:2, :], q2), c, *old, ns=520)
            kk = kst[:, z].rearrange("p h (r d) -> p h r d", d=16)
            h2 = act.do(lambda e: e.copy(
                kk[:, :, 0:4:3, :], rq[:, s, 16:20, :].unsqueeze(2).broadcast_to([P, 4, 2, 16])), c, *old, ns=200)
            pool.do(lambda e: e.tensor_tensor(qq[:, :, 1:4:2, :], q2, qq[:, :, 0:4:2, :].bitcast(F32),
                                              ALU.subtract), h1, ns=1225)
            qk_ok[i] = pool.do(lambda e: e.tensor_tensor(
                kk[:, :, 1:3, :], rq[:, s, 16:20, :].unsqueeze(2).broadcast_to([P, 4, 2, 16]),
                kk[:, :, 0:1, :].bitcast(F32).broadcast_to([P, 4, 2, 16]), ALU.subtract), h2, ns=417)
            rq_free[s] = [qk_ok[i]]

        def batch(b, banks, then=()):
            if b >= 1:
                yield blocked(lambda: xn_read[b - 1] is None or n_ok[b] is None, lambda: dve.t)
                norm(b)
            for p in range(2):
                bank = banks[p] if banks else None
                yield at([xn_ok[4 * b + 2 * p + 1]], bank)
                turn(2 * b + p, take(bank))
            for n in then:
                stats(n)
            for j in range(4):
                bank = banks[2 + j] if banks else None
                if b >= 2:
                    yield blocked(lambda: k_read[4 * (b - 2) + 3] is None, lambda: 0)
                yield at([xT_ok[4 * b + j]], bank)
                project(4 * b + j, take(bank))

        c_m = counts("m", 3)
        c_mt = [None] * 16
        st_read = [None] * 16
        pt_free = [[], [], []]
        npt = [0]
        o_ok = [None] * 16
        att_ok = [None] * 16


        mT_free = [[], []]

        dups, nm_ok = {}, {}

        def turn_qk(u):
            b, g, r = u // 4, u % 4, u % 3
            yield blocked(lambda: qk_ok[4 * b + 3] is None or (u >= 3 and st_read[u - 3] is None), lambda: 0)
            prior = [st_read[u - 3]] if u >= 3 else []
            got = []
            for hp in range(2):
                yield at([qk_ok[4 * b + 3]])
                bk = take()
                for tb in range(4):
                    z = (4 * b + tb) % 8
                    h = 4 * g + 2 * hp
                    src = qst[:, z, h:h + 2, :].rearrange("p h r -> p (h r)")
                    last = pe.do(lambda e, src=src, tb=tb, bk=bk: e.transpose(
                        ps[:, bk, tb * P:(tb + 1) * P].bitcast(F32R), src, idr[:]),
                        qk_ok[4 * b + tb], idr_ok, free[bk], ns=55)
                if hp == 1:
                    q_read[u] = last
                c1 = act.do(lambda e, hp=hp, bk=bk: e.copy(QS[0:64, r, 2 * hp, :], ps[0:64, bk, :]),
                            last, *prior, ns=478)
                c2 = dve.do(lambda e, hp=hp, bk=bk: e.tensor_copy(QS[0:64, r, 2 * hp + 1, :], ps[64:128, bk, :]),
                            last, *prior, ns=598)
                free[bk] = [c1, c2]
                got += [c1, c2]
            yield at([qk_ok[4 * b + 3]])
            bk = take()
            for tb in range(4):
                z = (4 * b + tb) % 8
                last = pe.do(lambda e, tb=tb, z=z, bk=bk: e.transpose(
                    ps[0:64, bk, tb * P:(tb + 1) * P].bitcast(F32R), kst[:, z, g, :], idr[:]), free[bk], ns=55)
            k_read[u] = last
            c1 = act.do(lambda e, bk=bk: e.copy(KS[0:64, r, :], ps[0:64, bk, :]), last, *prior, ns=478)
            free[bk] = [c1]
            dups[u] = got + [c1]

        def scores(u):
            r, w = u % 3, u % 2
            yield blocked(lambda: u not in dups or (u >= 2 and c_mt[u - 2] is None), lambda: 0)
            for tb in range(4):
                n = (tb + 1) * P
                per = 4 // (tb + 1) if tb < 2 else 1
                for h0 in range(0, 4, per):
                    yield at(dups[u])
                    bank = take()
                    view = ps[:, bank, 0:per * n].rearrange("p (j n) -> p j n", n=n)
                    mk = cmask[:].unsqueeze(1).broadcast_to([P, per, P])
                    pe.do(lambda e, view=view, mk=mk, n=n: e.matmul(
                        view[:, :, n - P:n], idb[:], mk, start=True, stop=True, skip_group_check=True),
                        sq_ok, free[bank], ns=max(per * 55, 107))
                    for j in range(per):
                        mm = pe.do(lambda e, j=j, h0=h0, tb=tb, n=n, bank=bank: e.matmul(
                            ps[:, bank, j * n:(j + 1) * n], QS[0:64, r, h0 + j, tb * P:(tb + 1) * P], KS[0:64, r, 0:n],
                            start=False, stop=True, skip_group_check=True), dups[u], ns=max(n / 2.4, 107))
                    d = dve.do(lambda e, view=view, tb=tb, h0=h0, per=per: e.tensor_reduce(
                        out=nm[:, w, tb, h0:h0 + per], in_=view, axis=AX, op=ALU.max, negate=True), mm,
                        ns=60 + per * n)
                    free[bank] = [d]
            mr = mhl[:, w]
            c = dve.do(lambda e: e.tensor_copy(mr[:, :, 0:4], nm[:, w]), d)
            c = dve.do(lambda e: e.tensor_tensor(mr[:, :, 4:8], nm[:, w], mr[:, :, 0:4].bitcast(F32), ALU.subtract), c)
            nm_ok[u] = c

        def shift(u):
            r, w = u % 3, u % 2
            yield blocked(lambda: u not in nm_ok, lambda: 0)
            c = nm_ok[u]
            yield at([c])
            bk = take()
            for tb in range(4):
                last = pe.do(lambda e, tb=tb, bk=bk: e.transpose(
                    ps[0:8, bk, tb * P:(tb + 1) * P].bitcast(F32R), mhl[:, w, tb, :], idr[:]), c, free[bk], ns=55)
            c = dve.do(lambda e, bk=bk: e.tensor_copy(mT[:, w, :], ps[0:8, bk, :]), last, mT_free[w], ns=598)
            free[bk] = [c]
            for half in range(2):
                c_mt[u] = sp.dma(lambda e, half=half: e.dma_start(
                    QS[64 + half:65 + half, r, :, :].bitcast(F32),
                    mT[4 * half:4 * half + 4, w, :]), c_m[r], c)
            mT_free[w] = [c_mt[u]]

        sel, chunk = {}, {}
        nw = [0]

        def attend(u):
            r = u % 3
            yield blocked(lambda: c_mt[u] is None, lambda: 0)
            for sb_ in range(4):
                n = 512 - sb_ * P
                chunk[u, sb_] = cs = npt[0] % 3
                yield blocked(lambda: nw[0] < npt[0] - 2, lambda: 0)
                npt[0] += 1
                nh = (1, 1, 2, 4)[sb_]
                for h0 in range(0, 4, nh):
                    yield at([c_mt[u]])
                    bk = take()
                    for j in range(nh):
                        mm = pe.do(lambda e, j=j, bk=bk, n=n, sb_=sb_, h0=h0: e.matmul(
                            ps[:, bk, j * n:(j + 1) * n], KS[0:66, r, sb_ * P:(sb_ + 1) * P],
                            QS[0:66, r, h0 + j, sb_ * P:512], start=True, stop=True),
                            free[bk], c_mt[u], k_one[r], ns=max(n / 2.4, 107))
                    ex = act.do(lambda e, bk=bk, cs=cs, h0=h0, nh=nh, n=n: e.activation(
                        PT[:, cs, h0:h0 + nh, 0:n], ps[:, bk, 0:nh * n].rearrange("p (h n) -> p h n", n=n),
                        ACT.Exp, scale=0.25), mm, pt_free[cs], ns=60 + nh * n * 0.83)
                    free[bk] = [ex]
                sel[u, sb_] = pool.do(lambda e, cs=cs: e.affine_select(
                    out=PT[:, cs, :, 0:P], in_=PT[:, cs, :, 0:P], pattern=[[0, 4], [1, P]],
                    compare_op=ALU.is_ge, fill=0.0, base=0, channel_multiplier=-1), ex, ns=594)
            st_read[u] = mm

        def weigh(u):
            b, g = u // 4, u % 4
            yield blocked(lambda: u >= 2 and att_ok[u - 2] is None, lambda: 0)
            for sb_ in range(4):
                yield blocked(lambda: (u, sb_) not in sel, lambda: 0)
                yield at([sel[u, sb_]], 6)
                n0 = sb_ * P
                cs = chunk[u, sb_]
                for h in range(4):
                    mm = pe.do(lambda e, h=h, n0=n0, cs=cs, sb_=sb_: e.matmul(
                        ps[32 * h:32 * h + 32, 6, n0:512], vaug[:, 4 * b + sb_, g, :], PT[:, cs, h, 0:512 - n0],
                        start=sb_ == 0, stop=sb_ == 3), sel[u, sb_], v_one, v_ok[4 * b + sb_], free[6],
                        ns=(512 - n0) * 5 / 3 / 4 + 20)
                pt_free[cs] = [mm]
                nw[0] += 1
            o_ok[u] = act.do(lambda e: e.copy(oT[:, u % 2, :], ps[:, 6, :]), mm, ns=478)
            free[6] = [o_ok[u]]

        def settle(u):
            b, g, w = u // 4, u % 4, u % 2
            yield blocked(lambda: o_ok[u] is None, lambda: 0)
            yield at([o_ok[u]])
            bk = take()
            for tb in range(4):
                last = pe.do(lambda e, tb=tb: e.transpose(
                    ps[:, bk, tb * P:(tb + 1) * P], oT[:, w, tb * P:(tb + 1) * P], idf[:]), o_ok[u], free[bk], ns=107)
            v = ps[:, bk, :].rearrange("p (t h d) -> p t h d", h=4, d=32)
            c = dve.do(lambda e: e.reciprocal(rd[:, w], v[:, :, :, 16]), last, ns=165)
            c = dve.do(lambda e: e.tensor_tensor(
                att[:, 4 * b:4 * b + 4, 64 * g:64 * g + 64].rearrange("p t (h d) -> p t h d", d=16),
                v[:, :, :, 0:16], rd[:, w].unsqueeze(3).broadcast_to([P, 4, 4, 16]), ALU.mult), c, ns=335)
            free[bk] = [c]
            att_ok[u] = c

        g_ok = []
        p_ok = []
        e_ok = []

        def route():
            yield blocked(lambda: qk_ok[NT - 1] is None, lambda: dve.t)
            dve.wait(qk_ok[NT - 1], qk_ok[NT - 2])
            for i in range(NT):
                c = dve.do(lambda e, i=i: e.max(out=m8[:, i, :], in_=lg[:, i, :]), lg_ok[i])
                if i % 4 == 3:
                    yield lambda: dve.t - 600
            for i in range(NT):
                c = dve.do(lambda e, i=i: e.max_index(out=i8[:, i, :], in_max=m8[:, i, :], in_values=lg[:, i, :]), c)
                if i % 4 == 3:
                    yield lambda: dve.t - 600
            yield lambda: dve.t - 600
            c1 = dve.do(lambda e: e.tensor_copy(ef[:, 0, :], i8[:, :, 0]), c)
            c1 = dve.do(lambda e: e.tensor_copy(ef[:, 1, :], i8[:, :, 1]), c)
            io16 = iof[:, 0:NE].unsqueeze(1).broadcast_to([P, NT, NE])
            for s in range(2):
                c = dve.do(lambda e, s=s: e.tensor_tensor(
                    A1[:, s], io16, ef[:, s, :].unsqueeze(2).broadcast_to([P, NT, NE]), ALU.is_equal), c1, k_ok, ns=335)
            ab = dve.do(lambda e: e.tensor_tensor(Ab[:], A1[:, 0], A1[:, 1], ALU.add), c)
            yield lambda: dve.t - 600
            c = dve.do(lambda e: e.tensor_tensor(
                lz[:], lg[:], m8[:, :, 0:1].broadcast_to([P, NT, NE]), ALU.subtract), c1, ns=335)
            c3 = dve.do(lambda e: e.tensor_tensor(e2[:], m8[:, :, 1], m8[:, :, 0], ALU.subtract), c)
            x1 = act.do(lambda e: e.activation(lz[:], lz[:], ACT.Exp), c3)
            x2 = act.do(lambda e: e.activation(e2[:], e2[:], ACT.Exp), c3)
            c = dve.do(lambda e: e.tensor_reduce(out=zz[:], in_=lz[:], axis=AX, op=ALU.add), x1)
            c = dve.do(lambda e: e.reciprocal(rz[:], zz[:]), c)
            dve.do(lambda e: e.tensor_copy(wv[:, 0, :], rz[:]), c)
            w_ok2 = dve.do(lambda e: e.tensor_tensor(wv[:, 1, :], e2[:], rz[:], ALU.mult), c, x2)
            yield at([ab])
            rb = take()
            cb = min((k for k in ring if k != rb), key=lambda k: ready(free[k]))
            pe.do(lambda e: e.matmul(ps[:, rb, 0:256], tri[:], Ab[:].rearrange("p i e -> p (i e)"),
                                     start=True, stop=True, skip_group_check=True), ab, sq_ok, free[rb])
            for i in range(NT - 1):
                n = NT - 1 - i
                rr = pe.do(lambda e, i=i, n=n: e.matmul(
                    ps[:, rb, 16 * (i + 1):256].rearrange("p (i e) -> p i e", e=NE), oneb[:],
                    Ab[:, i:i + 1, :].broadcast_to([P, n, NE]), start=False, stop=True,
                    skip_group_check=True), b_one)
            for i in range(NT):
                nn = pe.do(lambda e, i=i: e.matmul(ps[:, cb, 0:NE], oneb[:], Ab[:, i, :],
                                                   start=i == 0, stop=i == NT - 1), free[cb])
            c = dve.do(lambda e: e.tensor_copy(ne[:], ps[:, cb, 0:NE]), nn)
            free[cb] = [c]
            c = dve.do(lambda e: e.tensor_tensor(
                gt[:], ne[:].unsqueeze(2).broadcast_to([P, NE, NE]),
                iof[:, 48:64].unsqueeze(1).broadcast_to([P, NE, NE]), ALU.is_gt), c)
            c = dve.do(lambda e: e.tensor_reduce(out=nt[:], in_=gt[:], axis=AX, op=ALU.add), c)
            c = dve.do(lambda e: e.tensor_tensor(
                gt[:], tri16[:], nt[:].unsqueeze(1).broadcast_to([P, NE, NE]), ALU.mult), c)
            c = dve.do(lambda e: e.tensor_reduce(out=off[:], in_=gt[:], axis=AX, op=ALU.add), c)
            co = dve.do(lambda e: e.tensor_tensor(cend[:], off[:], nt[:], ALU.add), c)
            c = dve.do(lambda e: e.scalar_tensor_tensor(
                out=pe_[:], in0=off[:].unsqueeze(1).broadcast_to([P, NT, NE]), scalar=128.0,
                in1=ps[:, rb, 0:256].rearrange("p (i e) -> p i e", e=NE), op0=ALU.mult, op1=ALU.add), rr, c)
            free[rb] = [c]
            for s in range(2):
                c2 = dve.do(lambda e, s=s: e.tensor_tensor(pq[:, s], A1[:, s], pe_[:], ALU.mult), c)
            for s in range(2):
                c = dve.do(lambda e, s=s: e.tensor_reduce(out=posf[:, s, :], in_=pq[:, s], axis=AX, op=ALU.add), c2)
            c = dve.do(lambda e: e.tensor_copy(posu[:], posf[:].rearrange("p s i -> p (s i)")), c)
            c1 = dve.do(lambda e: e.tensor_scalar(ph[:], posu[:], 7, None, ALU.logical_shift_right), c)
            c1 = dve.do(lambda e: e.tensor_scalar(pl[:], posu[:], 127, None, ALU.bitwise_and), c)
            c = dve.do(lambda e: e.tensor_copy(phf[:], ph[:]), c1)
            c = dve.do(lambda e: e.tensor_copy(plf[:], pl[:]), c1)
            yield lambda: dve.t - 600
            k = dve.do(lambda e: e.tensor_tensor(
                ec[:], cend[0:1, :].unsqueeze(1).broadcast_to([1, NTILE, NE]),
                iof[0:1, 0:NTILE].unsqueeze(2).broadcast_to([1, NTILE, NE]), ALU.is_le), co, ns=852)
            yield lambda: dve.t - 600
            k = dve.do(lambda e: e.tensor_reduce(out=es[:], in_=ec[:], axis=AX, op=ALU.add), k, ns=852)
            k = dve.do(lambda e: e.tensor_scalar(es[:], es[:], float(NE - 1), None, ALU.min), k)
            dve.do(lambda e: e.tensor_scalar(eo[:, 0, :], es[:], float(4 * NI), None, ALU.mult), k)
            e_ok.append(dve.do(lambda e: e.tensor_scalar(eo[:, 1, :], es[:], float(2 * D), None, ALU.mult), k))
            yield lambda: dve.t - 600
            c4 = dve.do(lambda e: e.tensor_scalar(ph[:], posu[:], YR * P - 1, None, ALU.bitwise_and), c)
            c = dve.do(lambda e: e.tensor_copy(tokv[:], ph[:]), c4)
            c = dve.do(lambda e: e.tensor_tensor(tokv[:], tokc[:], tokv[:], ALU.subtract), c)
            used = [[], [], [], []]
            wf = wv[:].rearrange("p s i -> p (s i)")
            for n0 in range(0, 2 * NT, 2):
                yield lambda: dve.t - 600
                d = []
                for n in (n0, n0 + 1):
                    w = n % 4
                    dve.do(lambda e, n=n, w=w: e.tensor_scalar(
                        ohp[:, w, :], iota[:], plf[:, n:n + 1], None, ALU.is_equal), c, sq_ok, used[w], ns=196)
                    dve.do(lambda e, n=n, w=w: e.tensor_scalar(
                        oht[:, w, 0:NTILE], iota[:, 0:NTILE], phf[:, n:n + 1], tokv[:, n:n + 1],
                        ALU.is_equal, ALU.mult), ns=214)
                    d.append(dve.do(lambda e, n=n, w=w: e.tensor_scalar(
                        oht[:, w, NTILE:], iota[:, 0:NTILE], phf[:, n:n + 1], wf[:, n:n + 1],
                        ALU.is_equal, ALU.mult), w_ok2, ns=214))
                yield at(d)
                bank = take()
                for n in (n0, n0 + 1):
                    w = n % 4
                    mm = pe.do(lambda e, n=n, w=w, bank=bank: e.matmul(
                        ps[:, bank, 0:2 * NTILE], ohp[:, w, :], oht[:, w, :], start=n % 2 == 0, stop=n % 2 == 1,
                        skip_group_check=True), d[n % 2], free[bank], ns=157)
                    used[w] = [mm]
                if n0 == 0:
                    g1 = dve.do(lambda e, bank=bank: e.tensor_copy(gw[:], ps[:, bank, 0:2 * NTILE]), mm)
                else:
                    g1 = dve.do(lambda e, bank=bank: e.tensor_tensor(
                        gw[:], ps[:, bank, 0:2 * NTILE], gw[:], ALU.add), mm, g1)
                free[bank] = [g1]
            gf = gw[:, 0:NTILE]
            c = dve.do(lambda e: e.tensor_tensor(gf, gf, posc[:], ALU.add), g1)
            p_ok.append(dve.do(lambda e: e.tensor_copy(sidx[:], gf), c))
            g_ok.append(dve.do(lambda e: e.tensor_scalar(gidx[:], sidx[:], NB * T - 1, None, ALU.bitwise_and), p_ok[-1]))

        c_xr = counts("xr", 2)
        c_o = counts("o", 2)
        xr_free = [[], []]
        hh_free = [[], []]
        hT_free = [[], []]
        aT_free = [[], []]
        o_wr = [[], []]
        tiles = iter(range(NT))

        def share(w, ga, gb):
            for i in tiles:
                yield from shared(i, w, ga, gb)


        def shared(i, w, ga, gb):
            hb, ab = ga, gb
            yield blocked(lambda: att_ok[4 * (i // 4) + 3] is None, lambda: 0)
            ld = sp.dma(lambda e: e.dma_start(xr[:, w, :], a["x"][i * P:(i + 1) * P, :]), c_xr[w], xr_free[w])
            for half, bank in ((0, ga), (1, gb)):
                for k in range(2):
                    yield at([s_ok], bank)
                    mm = pe.do(lambda e, k=k, half=half, bank=bank: e.matmul(
                        ps[:, bank, 0:NS], xnT[:, k, i * P:(i + 1) * P], wsg[:, k, half * NS:(half + 1) * NS],
                        start=k == 0, stop=k == 1), s_ok, free[bank], ns=587)
                    if k == 1:
                        free[bank] = [mm]
            si = act.do(lambda e: e.activation(sg[:, w, :], ps[:, ga, 0:NS], ACT.Tanh, scale=0.5),
                        mm, hh_free[w], ns=344)
            m1 = dve.do(lambda e: e.scalar_tensor_tensor(
                out=sg[:, w, :], in0=sg[:, w, :], scalar=1.0, in1=ps[:, ga, 0:NS], op0=ALU.add, op1=ALU.mult),
                si, ns=435)
            mu = dve.do(lambda e: e.scalar_tensor_tensor(
                out=hh[:, w, :], in0=ps[:, gb, 0:NS], scalar=0.5, in1=sg[:, w, :],
                op0=ALU.mult, op1=ALU.mult), m1, hh_free[w], ns=435)
            free[ga], free[gb] = [m1], [mu]
            yield at([mu], hb)
            for k, n in enumerate(SH):
                last = pe.do(lambda e, k=k, n=n: e.transpose(
                    ps[0:n, hb, k * P:(k + 1) * P], hh[:, w, 128 * k:128 * k + n], idf[:]), mu, free[hb], ns=107)
            hh_free[w] = [last]
            c1 = act.do(lambda e: e.copy(hT[:, w, 0:2, :], ps[:, hb, 0:256].rearrange("p (k t) -> p k t", t=P)),
                        last, hT_free[w], ns=264)
            c1 = act.do(lambda e: e.copy(hT[0:96, w, 2, :], ps[0:96, hb, 256:384]), last, ns=158)
            free[hb] = [c1]
            yield at([att_ok[4 * (i // 4) + 3]], ab)
            for k in range(2):
                last = pe.do(lambda e, k=k: e.transpose(
                    ps[:, ab, k * P:(k + 1) * P], att[:, i, k * P:(k + 1) * P], idf[:]),
                    att_ok[4 * (i // 4) + 3], free[ab], ns=107)
            c2 = dve.do(lambda e: e.tensor_copy(aT[:, w], ps[:, ab, 0:256].rearrange("p (k t) -> p k t", t=P)),
                        last, aT_free[w], ns=331)
            for k, n in enumerate(SH):
                yield at([c1, c2], ab)
                pe.do(lambda e, k=k, n=n: e.matmul(
                    ps[:, ab, 256:512], hT[0:n, w, k, :], wsd[0:n, k, :], start=k == 0, stop=False), c1, c2, ns=427)
            for k in range(2):
                mm = pe.do(lambda e, k=k: e.matmul(ps[:, ab, 256:512], aT[:, w, k, :], wp[:, k, :],
                                                   start=False, stop=k == 1), ns=427)
            hT_free[w] = aT_free[w] = [mm]
            c = dve.do(lambda e: e.tensor_tensor(fo[:, w, :], ps[:, ab, 256:512], xr[:, w, :], ALU.add),
                       mm, ld, o_wr[w], ns=335)
            free[ab] = [c]
            xr_free[w] = [c]
            o_wr[w] = [sp.dma(lambda e: e.dma_start(a["out"][i * P:(i + 1) * P, :], fo[:, w, :]), c_o[w], c)]

        c_g = counts("g", XG)
        c_y = counts("y", YR)
        c_we = Count(sem("we"))
        xg_free = [[] for _ in range(XG)]
        gat = [None] * NTILE
        moe = [dict() for _ in range(NTILE)]
        y_wr = [None] * NTILE
        w_exp = []

        def load_up():
            for k in range(2):
                act.dma(lambda e, k=k: e.dma_start(
                    wgu[:, :, k, :], a["wgu"][:, P * k:P * k + P, :].rearrange("e p n -> p e n")), c_we)

        def load_down():
            for k in range(2):
                t = act.dma(lambda e, k=k: e.dma_start(
                    wdn[:, :, k, :], a["wdn"][:, HI * k:HI * k + HI, :].rearrange("e p n -> p e n")), c_we)
            w_exp.append(t)

        def gather(n):
            s = n % XG
            gat[n] = pool.dma(lambda e, n=n: e.indirect_dma_start(
                out=xg[:, s, :], out_offset=None, in_=xn_d,
                in_offset=bass.IndirectOffsetOnAxis(ap=gidx[:, n:n + 1], axis=0)), c_g[s], g_ok, xn_wr, xg_free[s])

        def moe_in(n):
            w, bank = n % 2, 2 + n % 2
            for k in range(2):
                last = pe.do(lambda e, k=k: e.transpose(
                    ps[:, bank, k * P:(k + 1) * P], xg[:, n % XG, k * P:(k + 1) * P], idf[:]), gat[n], free[bank])
            xg_free[n % XG] = [last]
            c = act.do(lambda e: e.copy(xgT[:, w], ps[:, bank, 0:256].rearrange("p (k t) -> p k t", t=P)), last)
            free[bank] = [c]
            moe[n]["x"] = c

        up_at = {}

        def up_load(e, n):
            return e.value_load(eo[0:1, 0, n:n + 1], min_val=0, max_val=(NE - 1) * 4 * NI)

        def moe_up(n):
            w, bank = n % 2, n % 2
            cell = {}

            def first(e):
                cell["v"] = up_at.pop(n) if n else up_load(e, n)
                return mul(e, 0)

            def mul(e, k):
                r = wgu[:].rearrange("p e k n -> p (e k n)")[:, bass.ds(cell["v"] + k * 2 * NI, 2 * NI)]
                return e.matmul(ps[:, bank, 0:2 * NI], xgT[:, w, k, :], r, start=k == 0, stop=k == 1)

            pe.do(first, e_ok, w_exp, moe[n]["x"], free[bank])

            def second(e):
                if n + 1 < NTILE:
                    up_at[n + 1] = up_load(e, n + 1)
                return mul(e, 1)

            mm = pe.do(second)
            si = act.do(lambda e: e.activation(sg[:, w, 0:NI], ps[:, bank, 0:NI], ACT.Silu), mm)
            mu = dve.do(lambda e: e.tensor_tensor(hh[:, w, 0:NI], sg[:, w, 0:NI], ps[:, bank, NI:2 * NI], ALU.mult), si)
            free[bank] = [mu]
            moe[n]["h"] = mu

        def moe_turn(n):
            w, bank = n % 2, 4 + n % 2
            for k in range(2):
                last = pe.do(lambda e, k=k: e.transpose(
                    ps[0:HI, bank, k * P:(k + 1) * P], hh[:, w, HI * k:HI * k + HI], idf[:]), moe[n]["h"], free[bank])
            c = dve.do(lambda e: e.tensor_copy(
                hT[0:HI, w, 0:2, :], ps[0:HI, bank, 0:256].rearrange("p (k t) -> p k t", t=P)), last)
            free[bank] = [c]
            moe[n]["t"] = c

        down_at = {}

        def down_load(e, n):
            return e.value_load(eo[0:1, 1, n:n + 1], min_val=0, max_val=(NE - 1) * 2 * D)

        def moe_down(n):
            w, bank, s = n % 2, 6 + n % 2, n % YR
            cell = {}

            def first(e):
                cell["v"] = down_at.pop(n) if n else down_load(e, n)
                return mul(e, 0)

            def second(e):
                if n + 1 < NTILE:
                    down_at[n + 1] = down_load(e, n + 1)
                return mul(e, 1)

            def mul(e, k):
                r = wdn[:].rearrange("p e k n -> p (e k n)")[:, bass.ds(cell["v"] + k * D, D)]
                return e.matmul(ps[:, bank, 0:D], hT[0:HI, w, k, :], r, start=k == 0, stop=k == 1)

            pe.do(first, moe[n]["t"], free[bank])
            mm = pe.do(second)
            prior = [y_wr[n - YR]] if n >= YR else []
            c = dve.do(lambda e: e.tensor_scalar(
                yo[:, s, :], ps[:, bank, 0:D], gw[:, NTILE + n:NTILE + n + 1], None, ALU.mult), mm, *prior)
            free[bank] = [c]
            moe[n]["y"] = c

        def scatter(n):
            s = n % YR
            before = [] if n else [z_wr, *o_wr[0], *o_wr[1]]
            y_wr[n] = pool.dma(lambda e: e.indirect_dma_start(
                out=a["out"], out_offset=bass.IndirectOffsetOnAxis(ap=sidx[:, n:n + 1], axis=0),
                in_=yo[:, s, :], in_offset=None, compute_op=ALU.add), c_y[s], p_ok, moe[n]["y"], before)

        def chain(*gens):
            for g in gens:
                yield from g

        zero_ok = pool.do(lambda e: e.memset(fo[:, 0, :], 0.0))
        z_wr = sp.dma(lambda e: e.dma_start(
            a["out"][NB * T:, :].rearrange("(i p) d -> p i d", p=P),
            fo[:, 0:1, :].broadcast_to([P, NT + YR, D])), c_z, zero_ok)

        def front():
            yield from batch(0, [7, 6, 4, 5, 0, 1], (1,))
            stats(2)
            stats(3)
            pt_free[2] = [n_ok[3]]
            yield from batch(1, None)
            load_x(3, xn_ok[7])
            yield from batch(2, None)
            yield from batch(3, None)

        def shifts():
            for u in range(16):
                yield from shift(u)
            yield lambda: ready(c_mt[15])
            act.wait(q_read[15], k_read[15], xn_ok[15], c_mt[15])
            load_up()

        stats(0)
        norm(0)
        k_one = [dve.do(lambda e, s=s: e.memset(KS[64:66, s, :].bitcast(F32), 1.0), ns=550) for s in range(3)]
        for n, t in enumerate((cmask, tri, iota)):
            sq_ok[:] = [dve.do(lambda e, n=n, t=t: e.tensor_copy(t[:], sq[:, n, :]), k_ok)]
        load_x(2, xn_ok[3])
        o_wr[0] = [z_wr]
        routing = route()
        lane = share(0, 2, 3)
        rest = order([chain(*[attend(u) for u in range(16)]), chain(*[weigh(u) for u in range(16)]),
                      chain(*[settle(u) for u in range(16)]), shifts(), routing,
                      chain(*[turn_qk(u) for u in range(16)]), front(), chain(*[scores(u) for u in range(16)]),
                      lane], 1, 1, 1, 1, 0, 1, 1, 1, 0)
        over = [st_read[15], q_read[15], k_read[15], *pt_free[0], *pt_free[1], *pt_free[2], xn_wr[3]]
        for eng in (sp, pool, act, dve):
            eng.wait(over)
        load_down()
        ring[:] = [4, 5, 6, 7]
        order([rest[4], rest[8], share(1, 0, 1)], 1, 1, 1)
        for n in range(XG):
            gather(n)
        moe_in(0)
        moe_in(1)
        for n in range(NTILE + 1):
            if n >= 1:
                moe_turn(n - 1)
            if n < NTILE:
                moe_up(n)
            if n >= 1:
                moe_down(n - 1)
                scatter(n - 1)
            if n + 2 < NTILE:
                moe_in(n + 2)
                if n + XG < NTILE:
                    gather(n + XG)
        c_f = Count(sem("f"))
        done = pool.dma(lambda e: e.dma_start(
            a["out"][0:NB * T, :].rearrange("(p i) d -> p i d", p=P),
            a["out"][NB * T:2 * NB * T, :].rearrange("(p i) d -> p i d", p=P), accum_op=ALU.add,
            max_dma_last_dim=8192), c_f, y_wr[-YR:])
        sp.wait(done)

        block = ctx.enter_context(nc.Block())
        block.sync(lambda e: sp.issue(e))
        block.gpsimd(lambda e: pool.issue(e))
        block.scalar(lambda e: act.issue(e))
        block.vector(lambda e: dve.issue(e))
        block.tensor(lambda e: pe.issue(e))


def constants():
    half = 8
    inv = (np.float32(1.0) / np.float32(10000.0) ** (np.arange(half, dtype=np.float32) / np.float32(half)))
    ang = np.arange(T, dtype=np.float32)[:, None] * inv.astype(np.float32)[None, :]
    cos, sin = np.cos(ang).astype(np.float32), np.sin(ang).astype(np.float32)
    cosv = np.concatenate([cos, cos], 1).reshape(4, P, 16).transpose(1, 0, 2)
    sinv = np.concatenate([-sin, sin], 1).reshape(4, P, 16).transpose(1, 0, 2)
    r = np.arange(P)
    iof = np.concatenate([np.arange(48), np.arange(16) * 128]).astype(np.float32)
    e = np.arange(NE)
    return {
        "idf": np.eye(P, dtype=np.float32),
        "sq": np.stack([np.where(r[None, :] > r[:, None], NEG, 0.0), r[:, None] < r[None, :],
                        np.broadcast_to(r, (P, P))], axis=1).astype(np.float32),
        "iof": np.broadcast_to(iof, (P, 64)).astype(np.float32),
        "tri16": np.broadcast_to((e[None, :] < e[:, None]), (P, NE, NE)).astype(np.float32),
        "posc": (r[:, None] + np.arange(NTILE) % YR * P + 2 * NB * T).astype(np.float32),
        "tokc": (r[:, None] + np.arange(2 * NT) * P - 2 * NB * T).astype(np.float32),
        "cosv": cosv,
        "sinv": sinv,
    }


def kernel(L0_attn_x, L0_attn_Wq, L0_attn_Wk, L0_attn_Wv, L0_attn_Wp, L0_ffn_gate_w, L0_ffn_w_gate_up,
           L0_ffn_w_down, L0_ffn_shared_gate_up, L0_ffn_shared_down):
    import concourse.bacc as bacc
    from concourse.bass_utils import run_bass_kernel_spmd

    f = np.asarray
    arrays = {
        "x": f(L0_attn_x).reshape(NB * T, D),
        "wcat": np.concatenate([f(L0_attn_Wq).T, f(L0_attn_Wk).T, f(L0_attn_Wv).T, f(L0_ffn_gate_w).T], axis=1),
        "wpT": f(L0_attn_Wp).T,
        "wgu": f(L0_ffn_w_gate_up),
        "wdn": f(L0_ffn_w_down),
        "wsg": f(L0_ffn_shared_gate_up),
        "wsd": f(L0_ffn_shared_down),
        **constants(),
    }
    nc = bacc.Bacc("TRN2", target_bir_lowering=False, num_devices=1)
    ins, aps = {}, {}
    for n, v in arrays.items():
        v = np.ascontiguousarray(v)
        ins["in_" + n] = v
        aps[n] = nc.dram_tensor("in_" + n, v.shape, mybir.dt.from_np(v.dtype), kind="ExternalInput").ap()
    aps["out"] = nc.dram_tensor("out_0", (2 * NB * T + YR * P, D), F32, kind="ExternalOutput").ap()
    build(nc, aps)
    r = run_bass_kernel_spmd(nc, [ins], core_ids=[0])
    return r.results[0]["out_0"][:NB * T].reshape(NB, T, D)
```
